# Optimizing a Trainium2 kernel written in Bass

```python
import numpy as np
import jax
import jax.numpy as jnp

def _softmax(x, axis=-1):
    return jax.nn.softmax(x, axis=axis)

def _gelu(x):
    return jax.nn.gelu(x, approximate=True)

def _silu(x):
    return jax.nn.silu(x)

def _sigmoid(x):
    return jax.nn.sigmoid(x)

def _layernorm(x, axis=-1, eps=1e-05):
    m = jnp.mean(x, axis=axis, keepdims=True)
    v = jnp.var(x, axis=axis, keepdims=True)
    return (x - m) / jnp.sqrt(v + eps)

def _scatter_add(tgt, idx, src, axis=0):
    return tgt.at[idx].add(src)

def _segment_sum(src, seg, n):
    return jax.ops.segment_sum(src, seg, n)
kernel_name = 'mk_recurrent_d1_jaxref_r4_699e76'

def setup_inputs(seed: int=0):
    np.random.seed(seed)
    _w = jnp.asarray

    def _L0_attn_setup():
        import jax, jax.numpy as jnp
        import numpy as np
        B, S, D = (2, 1024, 512)
        H, HKV, DH = (16, 4, 128)
        CHUNK = 64
        GROUPS = H // HKV

        def _alibi_slopes(n_heads):
            i = jnp.arange(1, n_heads + 1, dtype=jnp.float32)
            return jnp.exp2(-8.0 * i / n_heads)

        def _rope(x):
            s, d = (x.shape[2], x.shape[3])
            inv_freq = 1.0 / 10000.0 ** (jnp.arange(0, d, 2, dtype=jnp.float32) / d)
            freqs = jnp.arange(s, dtype=jnp.float32)[:, None] * inv_freq[None, :]
            cos = jnp.concatenate([jnp.cos(freqs), jnp.cos(freqs)], axis=-1)
            sin = jnp.concatenate([jnp.sin(freqs), jnp.sin(freqs)], axis=-1)
            x1, x2 = (x[..., :d // 2], x[..., d // 2:])
            rot = jnp.concatenate([-x2, x1], axis=-1)
            return x * cos[None, None] + rot * sin[None, None]

        def _lightning_attn(q, k, v):
            b, h, s, dh = q.shape
            nc = s // CHUNK
            lam = _alibi_slopes(h)
            r = jnp.arange(CHUNK, dtype=jnp.float32)
            diff = r[:, None] - r[None, :]
            diag = jnp.where(diff >= 0, jnp.exp(-lam[:, None, None] * diff), 0.0)
            q_dec = jnp.exp(-lam[:, None] * (r + 1.0))
            k_dec = jnp.exp(-lam[:, None] * (CHUNK - 1.0 - r))
            blk = jnp.exp(-lam * CHUNK)
            qc = q.reshape(b, h, nc, CHUNK, dh).transpose(2, 0, 1, 3, 4)
            kc = k.reshape(b, h, nc, CHUNK, dh).transpose(2, 0, 1, 3, 4)
            vc = v.reshape(b, h, nc, CHUNK, dh).transpose(2, 0, 1, 3, 4)

            def step(kv, inp):
                qi, ki, vi = inp
                scores = jnp.einsum('bhid,bhjd->bhij', qi, ki) * diag[None]
                o_intra = jnp.einsum('bhij,bhje->bhie', scores, vi)
                o_inter = jnp.einsum('bhid,bhde->bhie', qi * q_dec[None, :, :, None], kv)
                kv = blk[None, :, None, None] * kv + jnp.einsum('bhjd,bhje->bhde', ki * k_dec[None, :, :, None], vi)
                return (kv, o_intra + o_inter)
            kv0 = jnp.zeros((b, h, dh, dh), q.dtype)
            _, o = jax.lax.scan(step, kv0, (qc, kc, vc))
            return o.transpose(1, 2, 0, 3, 4).reshape(b, h, s, dh)
        key = jax.random.key(seed)
        ks = jax.random.split(key, 5)
        sc = 0.02
        return {'x': jax.random.normal(ks[0], (B, S, D), jnp.float32), 'wq': jax.random.normal(ks[1], (H * DH, D), jnp.float32) * sc, 'wk': jax.random.normal(ks[2], (HKV * DH, D), jnp.float32) * sc, 'wv': jax.random.normal(ks[3], (HKV * DH, D), jnp.float32) * sc, 'wo': jax.random.normal(ks[4], (D, H * DH), jnp.float32) * sc}
    _L0_attn_in = _L0_attn_setup()

    def _L0_ffn_setup():
        import jax, jax.numpy as jnp
        import numpy as np
        B, S, H, I = (1, 64, 512, 1536)

        def _quantized_matmul(x, w, scale):
            wq = w.astype(jnp.float8_e4m3fn).astype(x.dtype)
            y = jnp.einsum('bsi,io->bso', x, wq)
            return y * scale
        key = jax.random.key(seed)
        ks = jax.random.split(key, 7)
        return {'x': jax.random.normal(ks[0], (B, S, H), dtype=jnp.float32), 'gate_w': jax.random.normal(ks[1], (H, I), dtype=jnp.float32) * 0.02, 'up_w': jax.random.normal(ks[2], (H, I), dtype=jnp.float32) * 0.02, 'down_w': jax.random.normal(ks[3], (I, H), dtype=jnp.float32) * 0.02, 'gate_scale': jax.random.uniform(ks[4], (I,), dtype=jnp.float32, minval=0.5, maxval=1.5), 'up_scale': jax.random.uniform(ks[5], (I,), dtype=jnp.float32, minval=0.5, maxval=1.5), 'down_scale': jax.random.uniform(ks[6], (H,), dtype=jnp.float32, minval=0.5, maxval=1.5)}
    _L0_ffn_in = _L0_ffn_setup()
    _d = {'L0_attn_x': _L0_attn_in['x'], 'L0_attn_wq': _L0_attn_in['wq'], 'L0_attn_wk': _L0_attn_in['wk'], 'L0_attn_wv': _L0_attn_in['wv'], 'L0_attn_wo': _L0_attn_in['wo'], 'L0_ffn_gate_w': _L0_ffn_in['gate_w'], 'L0_ffn_up_w': _L0_ffn_in['up_w'], 'L0_ffn_down_w': _L0_ffn_in['down_w'], 'L0_ffn_gate_scale': _L0_ffn_in['gate_scale'], 'L0_ffn_up_scale': _L0_ffn_in['up_scale'], 'L0_ffn_down_scale': _L0_ffn_in['down_scale']}
    _x0 = _d['L0_attn_x']
    _d['L0_attn_x'] = jax.random.normal(jax.random.fold_in(jax.random.key(seed), 1), (4, 512, 512), dtype=_x0.dtype)
    del _x0
    return _d

def reference(L0_attn_x, L0_attn_wq, L0_attn_wk, L0_attn_wv, L0_attn_wo, L0_ffn_gate_w, L0_ffn_up_w, L0_ffn_down_w, L0_ffn_gate_scale, L0_ffn_up_scale, L0_ffn_down_scale):

    def _L0_attn_ref(x, wq, wk, wv, wo):
        import jax, jax.numpy as jnp
        import numpy as np
        B, S, D = (2, 1024, 512)
        H, HKV, DH = (16, 4, 128)
        CHUNK = 64
        GROUPS = H // HKV

        def _alibi_slopes(n_heads):
            i = jnp.arange(1, n_heads + 1, dtype=jnp.float32)
            return jnp.exp2(-8.0 * i / n_heads)

        def _rope(x):
            s, d = (x.shape[2], x.shape[3])
            inv_freq = 1.0 / 10000.0 ** (jnp.arange(0, d, 2, dtype=jnp.float32) / d)
            freqs = jnp.arange(s, dtype=jnp.float32)[:, None] * inv_freq[None, :]
            cos = jnp.concatenate([jnp.cos(freqs), jnp.cos(freqs)], axis=-1)
            sin = jnp.concatenate([jnp.sin(freqs), jnp.sin(freqs)], axis=-1)
            x1, x2 = (x[..., :d // 2], x[..., d // 2:])
            rot = jnp.concatenate([-x2, x1], axis=-1)
            return x * cos[None, None] + rot * sin[None, None]

        def _lightning_attn(q, k, v):
            b, h, s, dh = q.shape
            nc = s // CHUNK
            lam = _alibi_slopes(h)
            r = jnp.arange(CHUNK, dtype=jnp.float32)
            diff = r[:, None] - r[None, :]
            diag = jnp.where(diff >= 0, jnp.exp(-lam[:, None, None] * diff), 0.0)
            q_dec = jnp.exp(-lam[:, None] * (r + 1.0))
            k_dec = jnp.exp(-lam[:, None] * (CHUNK - 1.0 - r))
            blk = jnp.exp(-lam * CHUNK)
            qc = q.reshape(b, h, nc, CHUNK, dh).transpose(2, 0, 1, 3, 4)
            kc = k.reshape(b, h, nc, CHUNK, dh).transpose(2, 0, 1, 3, 4)
            vc = v.reshape(b, h, nc, CHUNK, dh).transpose(2, 0, 1, 3, 4)

            def step(kv, inp):
                qi, ki, vi = inp
                scores = jnp.einsum('bhid,bhjd->bhij', qi, ki) * diag[None]
                o_intra = jnp.einsum('bhij,bhje->bhie', scores, vi)
                o_inter = jnp.einsum('bhid,bhde->bhie', qi * q_dec[None, :, :, None], kv)
                kv = blk[None, :, None, None] * kv + jnp.einsum('bhjd,bhje->bhde', ki * k_dec[None, :, :, None], vi)
                return (kv, o_intra + o_inter)
            kv0 = jnp.zeros((b, h, dh, dh), q.dtype)
            _, o = jax.lax.scan(step, kv0, (qc, kc, vc))
            return o.transpose(1, 2, 0, 3, 4).reshape(b, h, s, dh)
        b, s, _ = x.shape
        q = jnp.einsum('bsd,ed->bse', x, wq).reshape(b, s, H, DH).transpose(0, 2, 1, 3)
        k = jnp.einsum('bsd,ed->bse', x, wk).reshape(b, s, HKV, DH).transpose(0, 2, 1, 3)
        v = jnp.einsum('bsd,ed->bse', x, wv).reshape(b, s, HKV, DH).transpose(0, 2, 1, 3)
        q = _rope(q)
        k = _rope(k)
        k = jnp.repeat(k, GROUPS, axis=1)
        v = jnp.repeat(v, GROUPS, axis=1)
        o = _lightning_attn(q, k, v)
        o = o.transpose(0, 2, 1, 3).reshape(b, s, H * DH)
        return jnp.einsum('bse,de->bsd', o, wo)

    def _L0_ffn_ref(x, gate_w, up_w, down_w, gate_scale, up_scale, down_scale):
        import jax, jax.numpy as jnp
        import numpy as np
        B, S, H, I = (1, 64, 512, 1536)

        def _quantized_matmul(x, w, scale):
            wq = w.astype(jnp.float8_e4m3fn).astype(x.dtype)
            y = jnp.einsum('bsi,io->bso', x, wq)
            return y * scale
        gate = jax.nn.silu(_quantized_matmul(x, gate_w, gate_scale))
        up = _quantized_matmul(x, up_w, up_scale)
        fuse = gate * up
        return _quantized_matmul(fuse, down_w, down_scale)
    x = L0_attn_x
    xn = _layernorm(x, axis=-1)
    s = _L0_attn_ref(xn, L0_attn_wq, L0_attn_wk, L0_attn_wv, L0_attn_wo)
    g = _silu(_L0_ffn_ref(xn, L0_ffn_gate_w, L0_ffn_up_w, L0_ffn_down_w, L0_ffn_gate_scale, L0_ffn_up_scale, L0_ffn_down_scale))
    x = x + s * g
    return x

_drawn_inputs = setup_inputs


def setup_inputs(seed=0):
    import zlib

    import numpy as np

    out = dict(_drawn_inputs(seed))
    spreads = {}
    factors = {}
    for name, (base, spread) in spreads.items():
        noise = np.random.default_rng([zlib.crc32(name.encode()), seed]).standard_normal(out[name].shape)
        drawn = base * np.exp(spread * noise) if base else spread * noise
        out[name] = jnp.asarray(drawn.astype(out[name].dtype))
    for name, factor in factors.items():
        out[name] = (out[name] * factor).astype(out[name].dtype)
    return out
```

```python
from contextlib import ExitStack

import concourse.bass as bass
from concourse import mybir

F32 = mybir.dt.float32
F32R = mybir.dt.float32r
I32 = mybir.dt.int32
ALU = mybir.AluOpType
ACT = mybir.ActivationFunctionType

P = 128
NB, S, D = 4, 512, 512
H, HKV, DH = 16, 4, 128
FF = 1536
EPS = 1e-5
KT = D // P
TT = S // P
MT = FF // P
NG = HKV
HG = H // HKV
PT = 2 + HG
ROT = DH // 2
BLOCKS = [(i, j) for i in range(TT) for j in range(i + 1)]
NBL = len(BLOCKS)
LAST = [max(t for t, (i, _) in enumerate(BLOCKS) if i == q) for q in range(TT)]
LAG = 3
SRING = 4
TRING = 3
QK = 1 + HG

EXP_MASK = 0x7F800000
F8_SCALE = 1.5 * 2.0**20
F8_FLOOR = 1.5 * 2.0**14


def attention_mlp_kernel(nc, x_nat, x_t, attn_w, out_w, mlp_w, scales, rope_tab, decay_tab, ident_in, out):
    ctx = ExitStack()
    with ctx:
        sem = lambda name: ctx.enter_context(nc.semaphore(name))

        def sb(name, shape, dt=F32, scope=ctx):
            return scope.enter_context(nc.sbuf_tensor(name, shape, dt))

        xn_dram = nc.dram_tensor("xn_split", (NB, P, 2, KT, S), F32, kind="Internal").ap()
        g_dram = nc.dram_tensor("mlp_gate", (KT, P, NB * S), F32, kind="Internal").ap()

        ident = sb("ident", [P, P])
        xn0 = sb("xn0", [P, 2, KT, S], F32R)
        stage = sb("stage", [P, PT * KT * P])
        base = nc.sbuf_base

        early = ExitStack()
        x_sb = sb("x_sb", [P, 2, TT, D], scope=early)
        xn_sb = sb("xn_sb", [P, 2, D], scope=early)
        magic = sb("magic", [P, 3 * KT * P], scope=early)
        nc_top_early = nc.sbuf_base
        early.close()
        aw = sb("aw", [P, 2, PT, KT, P], F32R)
        pad = nc_top_early - nc.sbuf_base
        if pad > 0:
            sb("pad", [P, pad // 4])

        mlp = ExitStack()
        xn123 = sb("xn123", [P, NB - 1, 2, KT, S], F32R, scope=mlp)
        gu_w = sb("gu_w", [P, MT, 3, KT, P], F32R, scope=mlp)
        sg = sb("sg", [P, 2, S], scope=mlp)
        fz = sb("fz", [P, 2, S], scope=mlp)
        fsplit = sb("fsplit", [P, 3, 2, S], F32R, scope=mlp)
        gout = sb("gout", [P, 2, S], scope=mlp)
        scale_sb = sb("scale_sb", [P, 2 * MT + KT], scope=mlp)
        stats = sb("stats", [P, TT, 6], scope=mlp)
        mv = sb("mv", [P, TT, 2], scope=mlp)
        rs = sb("rs", [P, 6, TT], scope=mlp)
        rstd = sb("rstd", [P, NB, TT], scope=mlp)
        nmr = sb("nmr", [P, NB, TT], scope=mlp)
        mlp.close()

        q_r = sb("q_r", [P, 2, HG, S], F32R)
        k_r = sb("k_r", [P, 2, S], F32R)
        v_r = sb("v_r", [P, 2, TT, DH], F32R)
        rot1 = sb("rot1", [P, 2, S])
        rot2 = sb("rot2", [P, 2, S])
        vt_sb = sb("vt_sb", [P, S])
        rope = sb("rope", [P, 2, S])
        ow = sb("ow", [P, 2, HG, D], F32R)
        o_r = sb("o_r", [P, 2, HG, S], F32R)
        s_sb = sb("s_sb", [P, TRING, HG, P])
        s_r = sb("s_r", [P, SRING, 2, HG, P], F32R)
        decay = sb("decay", [P, TT, HG, P])
        acc = sb("acc", [P, NB, KT, S])
        fin_in = sb("fin_in", [P, 2, 2, S])
        fin = sb("fin", [P, 2, S])

        bank = [ctx.enter_context(nc.psum_tensor(f"bank{i}", [P, 512], F32)) for i in range(8)]
        down_ps = bank[0:4]
        gu_ps = bank[4:7]
        ln_ps = bank[7]
        sc_ps = bank[0:3]
        o_ps = [bank[3], bank[6]]
        proj_ps = bank[4:6]
        vt_ps = bank[7]

        def xn_tb(tb, part, k):
            if isinstance(tb, int) and tb == 0:
                return xn0[:, part, k, :]
            return xn123[:, tb - 1, part, k, :]

        x_in = [sem("x_in0"), sem("x_in1")]; w_in = [sem("w_in0"), sem("w_in1")]; const_in = sem("const_in"); ident_sem = sem("ident_sem")
        stats_d = sem("stats_d"); var_d = sem("var_d"); pow_c = sem("pow_c"); pow_d = sem("pow_d"); newton = sem("newton")
        rstd_d = sem("rstd_d")
        normed = sem("normed"); ln_t = sem("ln_t"); ln_hi = sem("ln_hi"); ln_lo = sem("ln_lo")
        k_exp = sem("k_exp"); k_made = sem("k_made"); k_added = sem("k_added"); w_ready = sem("w_ready")
        gu_done = sem("gu_done"); silu_d = sem("silu_d"); f_d = sem("f_d"); f_hi = sem("f_hi"); f_lo = sem("f_lo")
        down_d = sem("down_d"); gate_d = sem("gate_d"); gate_out = [sem("gate_out0"), sem("gate_out1")]; xn_out = sem("xn_out")
        aw_in = sem("aw_in"); aw_hi = sem("aw_hi"); aw_lo = sem("aw_lo")
        ow_in = sem("ow_in"); ow_hi = sem("ow_hi"); ow_lo = sem("ow_lo")
        rope_in = sem("rope_in"); decay_in = sem("decay_in"); xn_in = sem("xn_in")
        zeroed = sem("zeroed")
        proj_d = sem("proj_d"); rot_d = sem("rot_d"); qk_sum = sem("qk_sum"); qk_hi = sem("qk_hi"); qk_lo = sem("qk_lo")
        vt_copied = sem("vt_copied"); vt_d = sem("vt_d"); v_hi = sem("v_hi"); v_lo = sem("v_lo")
        score_d = sem("score_d"); decayed = sem("decayed"); s_hi = sem("s_hi"); s_lo = sem("s_lo")
        pv_d = sem("pv_d"); o_hi = sem("o_hi"); o_lo = sem("o_lo")
        out_d = sem("out_d"); acc_d = sem("acc_d")
        fin_ld = [sem("fin_ld0"), sem("fin_ld1")]; fin_p = sem("fin_p"); fin_d = sem("fin_d"); stored = [sem("stored0"), sem("stored1")]

        block = ctx.enter_context(nc.Block())

        def run_steps(eng, group_start, step):
            with eng.Fori(0, NG - 1) as g:
                group_start(g)
                with eng.Fori(0, NB - 1) as b:
                    step(g * NB + b, g, b, b + 1, False, False, False)
                step(g * NB + (NB - 1), g, NB - 1, 0, True, False, False)
            g = NG - 1
            group_start(g)
            with eng.Fori(0, NB - 1) as b:
                step(b + g * NB, g, b, b + 1, False, True, False)
            step(g * NB + NB - 1, g, NB - 1, 0, False, True, True)

        @block.sync
        def _(sp):
            def load_x(tb):
                sp.dma_start(x_sb[:, tb % 2], x_nat[tb]).then_inc(x_in[tb % 2], 16)

            def load_w(m):
                if m >= 2:
                    sp.wait_ge(w_ready, m - 1)
                half = 3 * KT * P
                sp.dma_start(stage[:, (m % 2) * half:(m % 2 + 1) * half], mlp_w[m]).then_inc(w_in[m % 2], 16)

            def spill_xn(tb):
                sp.wait_ge(ln_lo, TT * (tb + 1))
                src = xn0[:] if tb == 0 else xn123[:, tb - 1]
                sp.dma_start(xn_dram[tb], src.bitcast(F32)).then_inc(xn_out, 16)

            load_x(0)
            sp.dma_start(ident[:], ident_in).then_inc(ident_sem, 16)
            load_w(0)
            load_w(1)
            load_x(1)
            sp.dma_start(scale_sb[:], scales).then_inc(const_in, 16)
            spill_xn(0)
            sp.wait_ge(normed, TT)
            load_x(2)
            for m in range(2, MT):
                load_w(m)
                if m == 6:
                    sp.wait_ge(normed, 2 * TT)
                    load_x(3)
                    spill_xn(1)
                if m == 10:
                    spill_xn(2)
            spill_xn(3)

            def load_aw(g):
                sp.dma_start(stage[:], attn_w[g]).then_inc(aw_in, 16)

            def store_gates(tb):
                for d in range(KT):
                    sp.wait_ge(gate_d, tb * KT + d + 1)
                    sp.dma_start(g_dram[d, :, bass.ts(tb, S)], gout[:, d % 2, :]).then_inc(gate_out[d % 2], 16)

            sp.wait_ge(w_ready, MT)
            load_aw(0)
            store_gates(0)
            with sp.Fori(1, NB) as tb:
                store_gates(tb)

            sp.dma_start(rope[:], rope_tab).then_inc(rope_in, 16)
            sp.dma_start(decay[:], decay_tab[0]).then_inc(decay_in, 16)
            sp.wait_ge(aw_lo, PT)
            sp.dma_start(stage[:, 0:HG * D], out_w[0]).then_inc(ow_in, 16)
            sp.wait_ge(xn_out, 16 * NB)
            for parity in range(2):
                sp.wait_ge(gate_out[parity], 8 * KT * NB)

            def group_start(g):
                if isinstance(g, int) and g == NG - 1:
                    return
                sp.wait_ge(ow_lo, g * HG + HG)
                sp.dma_start(stage[:], attn_w[g + 1]).then_inc(aw_in, 16)

            def step(n, g, b, b_next, edge, final, last):
                if not last:
                    sp.wait_ge(proj_d, n * PT + PT)
                    sp.dma_start(xn0[:].bitcast(F32), xn_dram[b_next]).then_inc(xn_in, 16)
                if edge:
                    sp.wait_ge(decayed, n * NBL + NBL)
                    sp.dma_start(decay[:], decay_tab[g + 1]).then_inc(decay_in, 16)
                    sp.wait_ge(aw_lo, g * PT + 2 * PT)
                    sp.dma_start(stage[:, 0:HG * D], out_w[g + 1]).then_inc(ow_in, 16)
                if final:
                    def load_fin(u):
                        sp.dma_start(fin_in[:, u % 2, 0, :], x_t[u, :, bass.ts(b, S)]).then_inc(fin_ld[u % 2], 16)
                        sp.dma_start(fin_in[:, u % 2, 1, :], g_dram[u, :, bass.ts(b, S)]).then_inc(fin_ld[u % 2], 16)

                    load_fin(0)
                    load_fin(1)
                    for u in range(KT):
                        sp.wait_ge(fin_d, b * KT + u + 1)
                        sp.dma_start(out[u, :, bass.ts(b, S)], fin[:, u % 2, :]).then_inc(stored[u % 2], 16)
                        if u + 2 < KT:
                            load_fin(u + 2)

            run_steps(sp, group_start, step)
            for parity in range(2):
                sp.wait_ge(stored[parity], 8 * KT * NB)

        @block.scalar
        def _(act):
            def norm(i):
                tb, j = divmod(i, TT)
                act.wait_ge(rstd_d, tb + 1)
                if i >= 2:
                    act.wait_ge(ln_t, i - 1)
                act.activation(xn_sb[:, i % 2, :], x_sb[:, tb % 2, j, :], ACT.Identity,
                               bias=nmr[:, tb, j:j + 1], scale=rstd[:, tb, j:j + 1]).then_inc(normed, 1)

            def norm_hi(i):
                tb, j = divmod(i, TT)
                act.wait_ge(ln_t, i + 1)
                dst = xn0[:, 0, :, bass.ts(j, P)] if tb == 0 else xn123[:, tb - 1, 0, :, bass.ts(j, P)]
                act.copy(dst, ln_ps[:].rearrange("p (k c) -> p k c", k=KT)).then_inc(ln_hi, 1)

            def silu_gate(tb, m):
                act.wait_ge(gu_done, tb * (2 * MT) + 2 * m + 1)
                if m >= 2 or not (isinstance(tb, int) and tb == 0):
                    act.wait_ge(f_d, tb * MT + m - 1)
                act.activation(sg[:, m % 2, :], gu_ps[(2 * m) % 3][:], ACT.Silu,
                               scale=scale_sb[:, m:m + 1]).then_inc(silu_d, 1)

            def fuse_hi(tb, m):
                act.wait_ge(f_d, tb * MT + m + 1)
                if m >= 3 or not (isinstance(tb, int) and tb == 0):
                    act.wait_ge(down_d, tb * MT + m - 2)
                act.copy(fsplit[:, m % 3, 0, :], fz[:, m % 2, :]).then_inc(f_hi, 1)

            def gates(tb):
                act.wait_ge(down_d, tb * MT + MT)
                for d in range(KT):
                    if d >= 2 or not (isinstance(tb, int) and tb == 0):
                        act.wait_ge(gate_out[d % 2], (tb * (KT // 2) + d // 2) * 16)
                    act.activation(gout[:, d % 2, :], down_ps[d][:], ACT.Silu,
                                   scale=scale_sb[:, 2 * MT + d:2 * MT + d + 1]).then_inc(gate_d, 1)

            for i in range(TT):
                norm(i)
                norm_hi(i)
            act.wait_ge(const_in, 16)
            for m in range(MT):
                norm(TT + m)
                silu_gate(0, m)
                fuse_hi(0, m)
                norm_hi(TT + m)
            gates(0)

            def aw_split_hi(g, t):
                act.wait_ge(aw_in, g * 16 + 16)
                act.copy(aw[:, 0, t, :, :], stage[:, bass.ts(t, KT * P)]).then_inc(aw_hi, 1)

            def ow_split_hi(g):
                act.wait_ge(ow_in, g * 16 + 16)
                for h in range(HG):
                    act.copy(ow[:, 0, h, :], stage[:, bass.ts(h, D)]).then_inc(ow_hi, 1)

            act.wait_ge(w_ready, MT)
            act.wait_ge(ln_t, NB * TT)
            for t in range(PT):
                aw_split_hi(0, t)
            with act.Fori(1, NB) as tb:
                for m in range(MT):
                    silu_gate(tb, m)
                    fuse_hi(tb, m)
                gates(tb)

            act.wait_ge(down_d, NB * MT)
            for parity in range(2):
                act.wait_ge(gate_out[parity], 8 * KT * NB)
            act.wait_ge(xn_out, 16 * NB)

            def qk_round(n, r):
                first = isinstance(n, int) and n == 0
                act.wait_ge(qk_sum, n * QK + r + 1)
                if not first:
                    act.wait_ge(score_d, n * NBL)
                dst = k_r[:, 0, :] if r == 0 else q_r[:, 0, r - 1, :]
                act.copy(dst, rot1[:, r % 2, :]).then_inc(qk_hi, 1)

            def copy_vt(n):
                act.wait_ge(proj_d, n * PT + 2)
                if not (isinstance(n, int) and n == 0):
                    act.wait_ge(vt_d, n)
                act.copy(vt_sb[:], proj_ps[1][:]).then_inc(vt_copied, 1)

            def v_round(n):
                act.wait_ge(vt_d, n + 1)
                if not (isinstance(n, int) and n == 0):
                    act.wait_ge(pv_d, n * NBL)
                act.copy(v_r[:, 0, :, :], vt_ps[:].rearrange("p (t e) -> p t e", t=TT)).then_inc(v_hi, 1)

            def projections(n, early=lambda: None):
                early()
                copy_vt(n)
                qk_round(n, 0)
                qk_round(n, 1)
                v_round(n)
                for r in range(2, QK):
                    qk_round(n, r)

            def o_round(n, i):
                act.wait_ge(pv_d, n * NBL + LAST[i] + 1)
                if not (isinstance(n, int) and n == 0) and i == 0:
                    act.wait_ge(out_d, n * KT)
                act.copy(o_r[:, 0, :, bass.ts(i, P)],
                         o_ps[i % 2][:].rearrange("p (h c) -> p h c", h=HG)).then_inc(o_hi, 1)

            def score_round(n, t):
                act.wait_ge(decayed, n * NBL + t + 1)
                if t >= SRING:
                    act.wait_ge(pv_d, n * NBL + t - SRING + 1)
                elif t == 0:
                    if_later(act, n, lambda: act.wait_ge(pv_d, n * NBL))
                act.copy(s_r[:, t % SRING, 0, :, :], s_sb[:, t % TRING, :, :]).then_inc(s_hi, 1)

            def step(n, g, b, b_next, edge, final, last):
                for t in range(NBL):
                    score_round(n, t)
                    if edge and 1 <= t <= PT:
                        aw_split_hi(g + 1, t - 1)
                    for i in range(TT):
                        if t == LAST[i] + LAG + 1:
                            o_round(n, i)
                for i in range(TT):
                    if LAST[i] + LAG + 1 >= NBL:
                        o_round(n, i)
                if not last:
                    projections(n + 1)
                if edge:
                    act.wait_ge(out_d, n * KT + KT)
                    ow_split_hi(g + 1)

            projections(0)
            ow_split_hi(0)
            run_steps(act, lambda g: None, step)

        @block.vector
        def _(dve):
            def mean_var(tb):
                dve.wait_ge(x_in[tb % 2], 16 * (tb // 2 + 1))
                if tb >= 1:
                    dve.wait_ge(rstd_d, tb)
                for j in range(TT):
                    dve.bn_stats(stats[:, j, :], x_sb[:, tb % 2, j, :]).then_inc(stats_d, 1)
                dve.wait_ge(stats_d, TT * (tb + 1))
                for j in range(TT):
                    dve.bn_aggr(mv[:, j, :], stats[:, j, :]).then_inc(newton, 1)
                dve.wait_ge(newton, 9 * tb + 4)
                dve.tensor_scalar(rs[:, 0, :], mv[:, :, 1], EPS, None, ALU.add).then_inc(var_d, 1)

            def inv_std(tb):
                dve.wait_ge(pow_d, tb + 1)
                c = 9 * tb + 4
                dve.tensor_tensor(rs[:, 3, :], rs[:, 2, :], rs[:, 2, :], ALU.mult).then_inc(newton, 1)
                dve.wait_ge(newton, c + 1)
                dve.tensor_tensor(rs[:, 4, :], rs[:, 3, :], rs[:, 0, :], ALU.mult).then_inc(newton, 1)
                dve.wait_ge(newton, c + 2)
                dve.tensor_scalar(rs[:, 5, :], rs[:, 4, :], -0.5, 1.5, ALU.mult, ALU.add).then_inc(newton, 1)
                dve.wait_ge(newton, c + 3)
                dve.tensor_tensor(rstd[:, tb, :], rs[:, 5, :], rs[:, 2, :], ALU.mult).then_inc(newton, 1)
                dve.wait_ge(newton, c + 4)
                dve.tensor_tensor(rs[:, 3, :], mv[:, :, 0], rstd[:, tb, :], ALU.mult).then_inc(newton, 1)
                dve.wait_ge(newton, c + 5)
                dve.tensor_scalar(nmr[:, tb, :], rs[:, 3, :], -1.0, None, ALU.mult).then_inc(rstd_d, 1)

            def norm_lo(i):
                tb, j = divmod(i, TT)
                dve.wait_ge(ln_hi, i + 1)
                parts = xn0 if tb == 0 else xn123[:, tb - 1]
                hi = parts[:, 0, :, bass.ts(j, P)]
                lo = parts[:, 1, :, bass.ts(j, P)]
                dve.tensor_tensor(lo, ln_ps[:].rearrange("p (k c) -> p k c", k=KT), hi.bitcast(F32),
                                  ALU.subtract).then_inc(ln_lo, 1)

            half = 3 * KT * P

            def w_magic(m):
                raw = stage[:, (m % 2) * half:(m % 2 + 1) * half]
                dve.wait_ge(w_in[m % 2], 16 * (m // 2 + 1))
                if m >= 1:
                    dve.wait_ge(w_ready, m)
                dve.tensor_scalar(magic[:].bitcast(I32), raw.bitcast(I32), EXP_MASK, None,
                                  ALU.bitwise_and).then_inc(k_exp, 1)
                dve.wait_ge(k_exp, m + 1)
                dve.tensor_scalar(magic[:], magic[:], F8_SCALE, F8_FLOOR, ALU.mult, ALU.max).then_inc(k_made, 1)

            def w_round(m):
                raw = stage[:, (m % 2) * half:(m % 2 + 1) * half]
                dve.wait_ge(k_added, m + 1)
                dve.tensor_tensor(gu_w[:, m, :, :, :], raw.rearrange("p (a k c) -> p a k c", a=3, k=KT),
                                  magic[:].rearrange("p (a k c) -> p a k c", a=3, k=KT),
                                  ALU.subtract).then_inc(w_ready, 1)

            def fuse(tb, m):
                dve.wait_ge(gu_done, tb * (2 * MT) + 2 * m + 2)
                dve.wait_ge(silu_d, tb * MT + m + 1)
                if m >= 2 or not (isinstance(tb, int) and tb == 0):
                    dve.wait_ge(f_lo, tb * MT + m - 1)
                dve.scalar_tensor_tensor(out=fz[:, m % 2, :], in0=gu_ps[(2 * m + 1) % 3][:],
                                         scalar=scale_sb[:, MT + m:MT + m + 1], in1=sg[:, m % 2, :],
                                         op0=ALU.mult, op1=ALU.mult).then_inc(f_d, 1)

            mean_var(0)
            w_magic(0)
            inv_std(0)
            w_round(0)
            mean_var(1)
            for i in range(TT):
                norm_lo(i)
            w_magic(1)
            inv_std(1)
            w_round(1)
            dve.wait_ge(const_in, 16)
            for m in range(MT):
                if m + 2 < MT:
                    w_magic(m + 2)
                if m % TT == 1 and m // TT + 2 < NB:
                    mean_var(m // TT + 2)
                fuse(0, m)
                norm_lo(TT + m)
                if m + 2 < MT:
                    w_round(m + 2)
                if m % TT == 2 and m // TT + 2 < NB:
                    inv_std(m // TT + 2)

            def aw_split_lo(g, t):
                dve.wait_ge(aw_hi, g * PT + t + 1)
                dve.tensor_tensor(aw[:, 1, t, :, :],
                                  stage[:, bass.ts(t, KT * P)].rearrange("p (k c) -> p k c", k=KT),
                                  aw[:, 0, t, :, :].bitcast(F32), ALU.subtract).then_inc(aw_lo, 1)

            def ow_split_lo(g):
                for h in range(HG):
                    dve.wait_ge(ow_hi, g * HG + h + 1)
                    dve.tensor_tensor(ow[:, 1, h, :], stage[:, bass.ts(h, D)],
                                      ow[:, 0, h, :].bitcast(F32), ALU.subtract).then_inc(ow_lo, 1)

            for t in range(PT):
                aw_split_lo(0, t)
            with dve.Fori(1, NB) as tb:
                for m in range(MT):
                    fuse(tb, m)

            dve.wait_ge(down_d, NB * MT)
            for parity in range(2):
                dve.wait_ge(gate_out[parity], 8 * KT * NB)
            dve.wait_ge(xn_out, 16 * NB)
            dve.wait_ge(rope_in, 16)

            def rotate(n, r):
                first = isinstance(n, int) and n == 0
                tile = 0 if r == 0 else r + 1
                ps = proj_ps[tile % 2]
                dve.wait_ge(proj_d, n * PT + tile + 1)
                if r >= 2:
                    dve.wait_ge(qk_lo, n * QK + r - 1)
                elif r == 0 and not first:
                    dve.wait_ge(qk_lo, n * QK)
                dve.tensor_tensor(rot1[:, r % 2, :], ps[:], rope[:, 0, :], ALU.mult)
                dve.tensor_tensor(rot2[0:ROT, r % 2, :], ps[ROT:, :], rope[0:ROT, 1, :], ALU.mult)
                dve.tensor_tensor(rot2[ROT:, r % 2, :], ps[0:ROT, :], rope[ROT:, 1, :], ALU.mult).then_inc(rot_d, 1)

            def v_rest(n):
                dve.wait_ge(v_hi, n + 1)
                dve.tensor_tensor(v_r[:, 1, :, :], vt_ps[:].rearrange("p (t e) -> p t e", t=TT),
                                  v_r[:, 0, :, :].bitcast(F32), ALU.subtract).then_inc(v_lo, 1)

            def projections(n, skip_first=False):
                if not skip_first:
                    rotate(n, 0)
                rotate(n, 1)
                rotate(n, 2)
                v_rest(n)
                for r in range(3, QK):
                    rotate(n, r)

            def decay_block(n, t):
                i, j = BLOCKS[t]
                dve.wait_ge(score_d, n * NBL + t + 1)
                if t >= TRING:
                    dve.wait_ge(s_lo, n * NBL + t - TRING + 1)
                elif t == 0:
                    if_later(dve, n, lambda: dve.wait_ge(s_lo, n * NBL))
                dve.tensor_tensor(s_sb[:, t % TRING, :, :], sc_ps[t % TRING][:].rearrange("p (h c) -> p h c", h=HG),
                                  decay[:, i - j, :, :], ALU.mult).then_inc(decayed, 1)

            def o_rest(n, i):
                dve.wait_ge(o_hi, n * TT + i + 1)
                dve.tensor_tensor(o_r[:, 1, :, bass.ts(i, P)], o_ps[i % 2][:].rearrange("p (h c) -> p h c", h=HG),
                                  o_r[:, 0, :, bass.ts(i, P)].bitcast(F32), ALU.subtract).then_inc(o_lo, 1)

            def accumulate(n, b, u):
                dve.wait_ge(out_d, n * KT + u + 1)
                dve.tensor_tensor(acc[:, b, u, :], proj_ps[u % 2][:], acc[:, b, u, :], ALU.add).then_inc(acc_d, 1)

            def finish(n, b, u):
                accumulate(n, b, u)
                dve.wait_ge(acc_d, n * KT + KT + u + 1)
                dve.wait_ge(fin_ld[u % 2], b * 64 + (u // 2 + 1) * 32)
                dve.tensor_tensor(fin_in[:, u % 2, 1, :], acc[:, b, u, :], fin_in[:, u % 2, 1, :],
                                  ALU.mult).then_inc(fin_p, 1)
                dve.wait_ge(fin_p, b * KT + u + 1)
                if u >= 2:
                    dve.wait_ge(stored[u % 2], (b * (KT // 2) + u // 2) * 16)
                else:
                    if_later(dve, b, lambda: dve.wait_ge(stored[u % 2], b * (KT // 2) * 16))
                dve.tensor_tensor(fin[:, u % 2, :], fin_in[:, u % 2, 1, :], fin_in[:, u % 2, 0, :],
                                  ALU.add).then_inc(fin_d, 1)

            def step(n, g, b, b_next, edge, final, last):
                dve.wait_ge(decay_in, g * 16 + 16)
                for t in range(NBL):
                    decay_block(n, t)
                    if edge and 1 <= t <= PT:
                        aw_split_lo(g + 1, t - 1)
                    for i in range(TT):
                        if t == LAST[i] + LAG + 1:
                            o_rest(n, i)
                if not last:
                    rotate(n + 1, 0)
                for i in range(TT):
                    if LAST[i] + LAG + 1 >= NBL:
                        o_rest(n, i)
                if not last:
                    projections(n + 1, skip_first=True)
                for u in range(KT):
                    if final:
                        finish(n, b, u)
                    else:
                        accumulate(n, b, u)
                if edge:
                    ow_split_lo(g + 1)

            projections(0)
            dve.wait_ge(zeroed, 1)
            dve.sem_inc(acc_d, KT)
            ow_split_lo(0)
            run_steps(dve, lambda g: None, step)

        @block.gpsimd
        def _(pool):
            pool.memset(rs[:, 1, :], -0.5).then_inc(pow_c, 1)
            pool.wait_ge(pow_c, 1)

            def power(tb):
                pool.wait_ge(var_d, tb + 1)
                if tb >= 1:
                    pool.wait_ge(rstd_d, tb)
                pool.tensor_tensor(rs[:, 2, :], rs[:, 0, :], rs[:, 1, :], ALU.pow).then_inc(pow_d, 1)

            half = 3 * KT * P

            def w_add(m):
                raw = stage[:, (m % 2) * half:(m % 2 + 1) * half]
                pool.wait_ge(k_made, m + 1)
                pool.tensor_tensor(raw, raw, magic[:], ALU.add).then_inc(k_added, 1)

            def fuse_rest(tb, m):
                pool.wait_ge(f_hi, tb * MT + m + 1)
                pool.tensor_tensor(fsplit[:, m % 3, 1, :], fz[:, m % 2, :], fsplit[:, m % 3, 0, :].bitcast(F32),
                                   ALU.subtract).then_inc(f_lo, 1)

            power(0)
            w_add(0)
            power(1)
            w_add(1)
            for m in range(MT):
                if m + 2 < MT:
                    w_add(m + 2)
                if m % TT == 1 and m // TT + 2 < NB:
                    power(m // TT + 2)
                fuse_rest(0, m)
            with pool.Fori(1, NB) as tb:
                for m in range(MT):
                    fuse_rest(tb, m)

            pool.wait_ge(down_d, NB * MT)
            for parity in range(2):
                pool.wait_ge(gate_out[parity], 8 * KT * NB)
            pool.wait_ge(xn_out, 16 * NB)

            def qk_add(n, r):
                pool.wait_ge(rot_d, n * QK + r + 1)
                pool.tensor_tensor(rot1[:, r % 2, :], rot1[:, r % 2, :], rot2[:, r % 2, :], ALU.add).then_inc(qk_sum, 1)

            def qk_rest(n, r):
                pool.wait_ge(qk_hi, n * QK + r + 1)
                dst, hi = (k_r[:, 1, :], k_r[:, 0, :]) if r == 0 else (q_r[:, 1, r - 1, :], q_r[:, 0, r - 1, :])
                pool.tensor_tensor(dst, rot1[:, r % 2, :], hi.bitcast(F32), ALU.subtract).then_inc(qk_lo, 1)

            def projections(n):
                qk_add(n, 0)
                for r in range(1, QK):
                    qk_add(n, r)
                    qk_rest(n, r - 1)
                qk_rest(n, QK - 1)

            def score_rest(n, t):
                pool.wait_ge(s_hi, n * NBL + t + 1)
                pool.tensor_tensor(s_r[:, t % SRING, 1, :, :], s_sb[:, t % TRING, :, :],
                                   s_r[:, t % SRING, 0, :, :].bitcast(F32), ALU.subtract).then_inc(s_lo, 1)

            def step(n, g, b, b_next, edge, final, last):
                for t in range(NBL):
                    score_rest(n, t)
                if not last:
                    projections(n + 1)

            projections(0)
            pool.memset(acc[:], 0.0).then_inc(zeroed, 1)
            run_steps(pool, lambda g: None, step)

        @block.tensor
        def _(pe):
            def products(dst, pairs, start=True, stop=True):
                for x, (a, b) in enumerate(pairs):
                    last = pe.matmul(dst, a, b, start=start and x == 0, stop=stop and x == len(pairs) - 1)
                return last

            def ln_transpose(i):
                pe.wait_ge(normed, i + 1)
                if i >= 1:
                    pe.wait_ge(ln_lo, i)
                for k in range(KT):
                    last = pe.transpose(ln_ps[:, bass.ts(k, P)], xn_sb[:, i % 2, bass.ts(k, P)], ident[:])
                last.then_inc(ln_t, 1)

            def gate_up(tb, m, s):
                q = 2 * m + s
                first = isinstance(tb, int) and tb == 0
                if not first or q >= 3:
                    was = q - 3
                    pe.wait_ge(f_d if was % 2 else silu_d, tb * MT + was // 2 + 1)
                products(gu_ps[q % 3][:], [(gu_w[:, m, s, k, :], xn_tb(tb, part, k))
                                           for part in range(2) for k in range(KT)]).then_inc(gu_done, 1)

            def down(tb, m):
                pe.wait_ge(f_lo, tb * MT + m + 1)
                if m == 0 and not (isinstance(tb, int) and tb == 0):
                    pe.wait_ge(gate_d, tb * KT)
                for d in range(KT):
                    last = products(down_ps[d][:], [(gu_w[:, m, 2, d, :], fsplit[:, m % 3, part, :]) for part in range(2)],
                                    start=(m == 0), stop=(m == MT - 1))
                last.then_inc(down_d, 1)

            pe.wait_ge(ident_sem, 16)
            for i in range(TT):
                ln_transpose(i)
            pe.wait_ge(ln_lo, TT)
            for m in range(MT):
                pe.wait_ge(w_ready, m + 1)
                gate_up(0, m, 0)
                gate_up(0, m, 1)
                ln_transpose(TT + m)
                if m >= 1:
                    down(0, m - 1)
            down(0, MT - 1)
            pe.wait_ge(ln_lo, NB * TT)
            with pe.Fori(1, NB) as tb:
                for m in range(MT):
                    gate_up(tb, m, 0)
                    gate_up(tb, m, 1)
                    if m >= 1:
                        down(tb, m - 1)
                down(tb, MT - 1)

            SPLIT = [(0, 0), (0, 1), (1, 0)]

            def project(n, tile, g_edge=None):
                first = isinstance(n, int) and n == 0
                if g_edge is not None:
                    pe.wait_ge(aw_lo, g_edge * PT + tile + 1)
                if tile == 0 and not first:
                    pe.wait_ge(xn_in, n * 16)
                if tile < 2:
                    if not first:
                        pe.wait_ge(acc_d, (n - 1) * KT + 3 + tile)
                elif tile == 3:
                    pe.wait_ge(vt_copied, n + 1)
                else:
                    pe.wait_ge(rot_d, n * QK + max(tile - 2, 1))
                products(proj_ps[tile % 2][:], [(aw[:, a, tile, k, :], xn0[:, c, k, :])
                                                for a, c in SPLIT for k in range(KT)]).then_inc(proj_d, 1)

            def transpose_v(n):
                pe.wait_ge(vt_copied, n + 1)
                if not (isinstance(n, int) and n == 0):
                    pe.wait_ge(v_lo, n)
                for j in range(TT):
                    last = pe.transpose(vt_ps[:, bass.ts(j, P)], vt_sb[:, bass.ts(j, P)], ident[:])
                last.then_inc(vt_d, 1)

            def projections(n, g_edge=None, skip_first=False):
                for tile in range(skip_first, PT):
                    project(n, tile, g_edge)
                    if tile == 3:
                        transpose_v(n)

            def scores(n, t):
                i, j = BLOCKS[t]
                if t >= TRING:
                    pe.wait_ge(decayed, n * NBL + t - TRING + 1)
                elif t == 0:
                    pe.wait_ge(qk_lo, n * QK + QK)
                    if_later(pe, n, lambda: pe.wait_ge(decayed, n * NBL))
                products(sc_ps[t % TRING][:], [(k_r[:, a, bass.ts(j, P)], q_r[:, c, :, bass.ts(i, P)])
                                               for a, c in SPLIT]).then_inc(score_d, 1)

            def times_v(n, t):
                i, j = BLOCKS[t]
                if t == 0:
                    pe.wait_ge(v_lo, n + 1)
                if j == 0:
                    if i >= 2:
                        pe.wait_ge(o_lo, n * TT + i - 1)
                    elif i == 0:
                        if_later(pe, n, lambda: pe.wait_ge(o_lo, n * TT))
                pe.wait_ge(s_lo, n * NBL + t + 1)
                products(o_ps[i % 2][:], [(v_r[:, a, j, :], s_r[:, t % SRING, c, :, :]) for a, c in SPLIT],
                         start=(j == 0), stop=(j == i)).then_inc(pv_d, 1)

            def out_projection(n, g, u, last):
                if u >= 2 or last:
                    pe.wait_ge(acc_d, n * KT + KT + u - 1)
                else:
                    pe.wait_ge(rot_d, n * QK + 2 * QK + u - 1)
                products(proj_ps[u % 2][:], [(ow[:, a, h, bass.ts(u, P)], o_r[:, c, h, :])
                                             for h in range(HG) for a, c in SPLIT]).then_inc(out_d, 1)

            def step(n, g, b, b_next, edge, final, last):
                g_edge = g + 1 if edge else None
                for t in range(NBL + LAG):
                    if t < NBL:
                        scores(n, t)
                    if t == NBL and not last:
                        project(n + 1, 0, g_edge)
                    if t >= LAG:
                        times_v(n, t - LAG)
                if not last:
                    projections(n + 1, g_edge, skip_first=True)
                pe.wait_ge(o_lo, n * TT + TT)
                pe.wait_ge(ow_lo, g * HG + HG)
                for u in range(KT):
                    out_projection(n, g, u, last)

            pe.wait_ge(silu_d, NB * MT)
            pe.wait_ge(f_d, NB * MT)
            projections(0, 0)
            pe.wait_ge(gate_d, NB * KT)
            run_steps(pe, lambda g: None, step)


def if_later(eng, n, wait):
    if not isinstance(n, int) or n > 0:
        wait()


def _constants():
    import numpy as np
    f = np.float32
    inv = f(1.0) / np.power(f(10000.0), np.arange(0, DH, 2, dtype=f) / f(DH)).astype(f)
    angle = (np.arange(S, dtype=f)[:, None] * inv[None, :]).astype(f).T.astype(np.float64)
    cos, sin = np.cos(angle), np.sin(angle)
    rope = np.stack([np.concatenate([cos, cos]), np.concatenate([-sin, sin])], axis=1).astype(f)
    lam = np.exp2(-8.0 * np.arange(1, H + 1, dtype=np.float64) / H)
    j = np.arange(P)[:, None, None]
    dist = P * np.arange(TT)[None, :, None] + np.arange(P)[None, None, :] - j
    table = np.where(dist >= 0, np.exp(-lam[:, None, None, None] * np.maximum(dist, 0)), 0.0)
    decay = table.reshape(NG, HG, P, TT, P).transpose(0, 2, 3, 1, 4).astype(f)
    return rope, np.ascontiguousarray(decay), np.eye(P, dtype=f)


def kernel(L0_attn_x, L0_attn_wq, L0_attn_wk, L0_attn_wv, L0_attn_wo, L0_ffn_gate_w, L0_ffn_up_w, L0_ffn_down_w,
           L0_ffn_gate_scale, L0_ffn_up_scale, L0_ffn_down_scale):
    import numpy as np
    import concourse.bacc as bacc
    from concourse.bass_utils import run_bass_kernel_spmd

    c = np.ascontiguousarray
    x = np.asarray(L0_attn_x)
    x_nat = c(x.reshape(NB, TT, P, D).transpose(0, 2, 1, 3))
    x_t = c(x.reshape(NB * S, KT, P).transpose(1, 2, 0))
    wq = np.asarray(L0_attn_wq).reshape(NG, HG, DH, KT, P)
    wk = np.asarray(L0_attn_wk).reshape(NG, 1, DH, KT, P)
    wv = np.asarray(L0_attn_wv).reshape(NG, 1, DH, KT, P)
    attn_w = c(np.concatenate([wk, wv, wq], axis=1).transpose(0, 4, 1, 3, 2).reshape(NG, P, PT * KT * P))
    out_w = c(np.asarray(L0_attn_wo).reshape(D, NG, HG, P).transpose(1, 3, 2, 0).reshape(NG, P, HG * D))
    gu = [np.asarray(w).reshape(KT, P, MT, P).transpose(2, 1, 0, 3) for w in (L0_ffn_gate_w, L0_ffn_up_w)]
    dw = np.asarray(L0_ffn_down_w).reshape(MT, P, KT, P)
    mlp_w = c(np.stack(gu + [dw], axis=2).reshape(MT, P, 3 * KT * P))
    scales = c(np.concatenate([np.asarray(L0_ffn_gate_scale).reshape(MT, P), np.asarray(L0_ffn_up_scale).reshape(MT, P),
                               np.asarray(L0_ffn_down_scale).reshape(KT, P)]).T)
    rope, decay, ident = _constants()
    arrays = {"x_nat": x_nat, "x_t": x_t, "attn_w": attn_w, "out_w": out_w, "mlp_w": mlp_w, "scales": scales,
              "rope": rope, "decay": decay, "ident": ident}

    nc = bacc.Bacc("TRN2", target_bir_lowering=False, num_devices=1)
    args = [nc.dram_tensor(f"in_{k}", a.shape, F32, kind="ExternalInput").ap() for k, a in arrays.items()]
    out = nc.dram_tensor("out_t", (KT, P, NB * S), F32, kind="ExternalOutput").ap()
    attention_mlp_kernel(nc, *args, out)
    r = run_bass_kernel_spmd(nc, [{f"in_{k}": a for k, a in arrays.items()}], core_ids=[0])
    got = r.results[0]["out_t"]
    return got.reshape(D, NB, S).transpose(1, 2, 0)
```

```python
from contextlib import ExitStack

import concourse.bass as bass
from concourse import mybir

F32 = mybir.dt.float32
F32R = mybir.dt.float32r
I32 = mybir.dt.int32
ALU = mybir.AluOpType
ACT = mybir.ActivationFunctionType

P = 128
NB, S, D = 4, 512, 512
H, HKV, DH = 16, 4, 128
FF = 1536
EPS = 1e-5
KT = D // P
TT = S // P
MT = FF // P
NG = HKV
HG = H // HKV
PT = 2 + HG
ROT = DH // 2
HALF = S // 2
BLOCKS = [(3, 0, HG, 3, 1), (2, 0, 2, 2, 2), (2, 2, 2, 2, 2), (0, 0, HG, 1, 1), (1, 0, HG, 1, 1), (0, 0, HG, 0, 1)]
NBL = len(BLOCKS)
OTILES = [(slice(0, 2), slice(HALF, S)), (slice(2, 4), slice(HALF, S)),
          (slice(0, HG), slice(P, 2 * P)), (slice(0, HG), slice(0, P))]
ODONE = [1, 2, 4, 5]
OF_BLOCK = [None, 0, 1, 2, 2, 3]
NOT = len(OTILES)
LAG = 3
VD = HALF // P
QD = HG // 2
SC = VD + QD
NEL = SC + NBL
NDEC = VD + NBL
SRING = 5
HEAD = 3
RRING = 3
FINR = 3
FLAG = 2
FRING = FLAG + 1
PARTS = 3
NPARTS = MT * PARTS
WRING = 6
MRING = 3
MLEAD = MRING - 1

LN_AT = {(0, m): TT + m // 2 - 2 for m in (4, 6, 8, 10)} | {(1, m): 2 * TT + m - 1 for m in range(1, 2 * TT + 1)}
AW_AT = {(1, m): (2 * (m - 8), 2 * (m - 8) + 1) for m in (8, 9, 10)}
TRING = 3
QK = 1 + HG

EXP_MASK = 0x7F800000
F8_SCALE = 1.5 * 2.0**20
F8_FLOOR = 1.5 * 2.0**14


def attention_mlp_kernel(nc, x_nat, x_t, attn_w, out_w, mlp_w, scales, rope_tab, decay_tab, q_decay_tab, k_decay_tab, ident_in, out):
    ctx = ExitStack()
    with ctx:
        sem = lambda name: ctx.enter_context(nc.semaphore(name))

        def sb(name, shape, dt=F32, scope=ctx):
            return scope.enter_context(nc.sbuf_tensor(name, shape, dt))

        xn_dram = nc.dram_tensor("xn_split", (NB, P, 2, KT, S), F32, kind="Internal").ap()
        g_dram = nc.dram_tensor("mlp_gate", (KT, P, NB * S), F32, kind="Internal").ap()

        ident = sb("ident", [P, P])
        k_decay = sb("k_decay", [P, NG, VD, HG])
        xn0 = sb("xn0", [P, 2, KT, S], F32R)
        stage = sb("stage", [P, WRING, KT * P])
        early = ExitStack()
        x_sb = sb("x_sb", [P, 2, TT, D], scope=early)
        magic = sb("magic", [P, MRING, KT * P], scope=early)
        early_end = nc.sbuf_base
        early.close()
        aw = sb("aw", [P, 2, PT, KT, P], F32R)
        rope = sb("rope", [P, 2, S])
        assert nc.sbuf_base >= early_end

        mlp = ExitStack()
        xn123 = sb("xn123", [P, NB - 1, 2, KT, S], F32R, scope=mlp)
        gu_w = sb("gu_w", [P, MT, 3, KT, P], F32R, scope=mlp)
        fz = sb("fz", [P, 2, S], scope=mlp)
        fsplit = sb("fsplit", [P, FRING, 2, S], F32R, scope=mlp)
        gout = sb("gout", [P, KT, S], scope=mlp)
        scale_sb = sb("scale_sb", [P, 2 * MT + KT], scope=mlp)
        stats = sb("stats", [P, TT, 6], scope=mlp)
        mv = sb("mv", [P, TT, 2], scope=mlp)
        rs = sb("rs", [P, 6, TT], scope=mlp)
        rstd = sb("rstd", [P, NB, TT], scope=mlp)
        nmr = sb("nmr", [P, NB, TT], scope=mlp)
        mlp.close()

        q_r = sb("q_r", [P, 2, HG, S], F32R)
        k_r = sb("k_r", [P, 2, S], F32R)
        kn_r = sb("kn_r", [P, 2, VD, DH], F32R)
        v_r = sb("v_r", [P, 2, TT, DH], F32R)
        ow = sb("ow", [P, 2, HG, D], F32R)
        vt_sb = sb("vt_sb", [P, S])
        d_sb = sb("d_sb", [P, SRING, S])
        d_r = sb("d_r", [P, SRING, 2, S], F32R)
        o_r = sb("o_r", [P, 2, HG, S], F32R)
        acc = sb("acc", [P, NB, KT, S])
        rot1 = sb("rot1", [P, RRING, S])
        rot2 = sb("rot2", [P, RRING, S])
        st_r = sb("st_r", [P, 2, HG, DH], F32R)
        decay = sb("decay", [P, HG, 2, P])
        q_decay = sb("q_decay", [P, HG, HALF])
        fin = sb("fin", [P, 2, S])
        fin_in = stage[:].rearrange("p (r t) s -> p r t s", t=2)

        bank = [ctx.enter_context(nc.psum_tensor(f"bank{i}", [P, 512], F32)) for i in range(8)]
        down_ps = bank[0:4]
        gu_ps = bank[4:7]
        sc_ps = bank[0:3]
        o_ps = [bank[3], bank[6], bank[7], bank[3]]
        inter_ps = o_ps[0:2]
        proj_ps = [bank[4], bank[5], bank[0], bank[1], bank[2], bank[4]]
        out_ps = [bank[5], bank[0], bank[4], bank[5]]
        st_ps = bank[3]

        def is_first(n):
            return isinstance(n, int) and n == 0

        def proj_bank(n, tile):
            return ([bank[4], bank[5], bank[6], bank[0], bank[1], bank[2]] if is_first(n) else proj_ps)[tile]

        def vt_bank(n):
            return bank[7] if is_first(n) else bank[6]

        def kt_bank(n):
            return bank[3] if is_first(n) else bank[7]

        def xn_tb(tb, part, k):
            if isinstance(tb, int) and tb == 0:
                return xn0[:, part, k, :]
            return xn123[:, tb - 1, part, k, :]

        x0_in = [sem(f"x0_in{i}") for i in range(TT)]; x_in = [sem("x_in0"), sem("x_in1")]; w_in = [sem(f"w_in{i}") for i in range(WRING)]; const_in = sem("const_in"); ident_sem = sem("ident_sem")
        stats_d = sem("stats_d"); var_d = sem("var_d"); pow_c = sem("pow_c"); pow_d = sem("pow_d"); newton = sem("newton")
        rstd_d = sem("rstd_d")
        normed = sem("normed"); ln_t = sem("ln_t"); ln_hi = sem("ln_hi"); ln_lo = sem("ln_lo")
        k_exp = sem("k_exp"); k_made = sem("k_made"); k_added = sem("k_added"); w_ready = sem("w_ready")
        gu_done = sem("gu_done"); silu_d = sem("silu_d"); f_d = sem("f_d"); f_hi = sem("f_hi"); f_lo = sem("f_lo")
        down_d = sem("down_d"); gate_d = sem("gate_d"); gate_out = sem("gate_out"); xn_out = sem("xn_out")
        aw_in = sem("aw_in"); aw_hi = sem("aw_hi"); aw_lo = sem("aw_lo")
        ow_in = sem("ow_in"); ow_hi = sem("ow_hi"); ow_lo = sem("ow_lo")
        rope_in = sem("rope_in"); decay_in = sem("decay_in"); k_decay_in = sem("k_decay_in"); xn_in = sem("xn_in")
        zeroed = sem("zeroed")
        proj_d = sem("proj_d"); turned = sem("turned"); rot_d = sem("rot_d"); qk_sum = sem("qk_sum"); qk_hi = sem("qk_hi"); qk_lo = sem("qk_lo")
        vt_copied = sem("vt_copied"); vt_d = sem("vt_d"); v_hi = sem("v_hi"); v_lo = sem("v_lo")
        kt_d = sem("kt_d"); kn_hi = sem("kn_hi"); kn_lo = sem("kn_lo")
        st_hi = sem("st_hi"); st_lo = sem("st_lo"); 
        score_d = sem("score_d"); decayed = sem("decayed"); q_decayed = sem("q_decayed"); d_hi = sem("d_hi"); d_lo = sem("d_lo")
        d_used = sem("d_used"); o_hi = sem("o_hi"); o_lo = sem("o_lo")
        out_d = sem("out_d"); acc_d = sem("acc_d")
        fin_ld = [sem(f"fin_ld{i}") for i in range(FINR)]; fin_p = sem("fin_p"); fin_d = sem("fin_d"); stored = [sem("stored0"), sem("stored1")]

        block = ctx.enter_context(nc.Block())

        def ln_ps(i):
            return down_ps[i] if i < TT else bank[7]

        def run_steps(eng, step):
            def group(g, final):
                step(g * NB, g, 0, start=True, final=final)
                with eng.Fori(1, NB - 1) as b:
                    step(b + g * NB, g, b, final=final)
                step(g * NB + (NB - 1), g, NB - 1, edge=not final, final=final, last=final)

            with eng.Fori(0, NG - 1) as g:
                group(g, False)
            group(NG - 1, True)

        @block.sync
        def _(sp):
            def load_x(tb):
                sp.dma_start(x_sb[:, tb % 2], x_nat[tb]).then_inc(x_in[tb % 2], 16)

            def load_w(q):
                if q >= WRING:
                    sp.wait_ge(w_ready, q - WRING + 1)
                sp.dma_start(stage[:, q % WRING, :], mlp_w[q // PARTS, :, q % PARTS, :]).then_inc(w_in[q % WRING], 16)

            def spill_xn(tb):
                sp.wait_ge(ln_lo, TT * (tb + 1))
                src = xn0[:] if tb == 0 else xn123[:, tb - 1]
                sp.dma_start(xn_dram[tb], src.bitcast(F32)).then_inc(xn_out, 16)

            def store_gates(tb):
                for d in range(KT):
                    sp.wait_ge(gate_d, tb * KT + d + 1)
                    sp.dma_start(g_dram[d, :, bass.ts(tb, S)], gout[:, d, :]).then_inc(gate_out, 16)

            def load_decay(g):
                sp.dma_start(decay[:], decay_tab[g]).then_inc(decay_in, 16)
                sp.dma_start(q_decay[:], q_decay_tab[g]).then_inc(decay_in, 16)

            def load_aw(g):
                sp.dma_start(stage[:], attn_w[g]).then_inc(aw_in, 16)

            for j in range(TT):
                sp.dma_start(x_sb[:, 0, j, :], x_nat[0, :, j, :]).then_inc(x0_in[j], 16)
            sp.dma_start(ident[:], ident_in).then_inc(ident_sem, 16)
            for q in range(3):
                load_w(q)
            sp.dma_start(scale_sb[:], scales).then_inc(const_in, 16)
            sp.dma_start(k_decay[:], k_decay_tab).then_inc(k_decay_in, 16)
            load_x(1)
            for q in range(3, NPARTS):
                load_w(q)
                if q == 8:
                    sp.wait_ge(ln_t, TT)
                    load_x(2)
                if q == 10:
                    spill_xn(0)
            spill_xn(1)
            load_x(3)
            spill_xn(2)
            store_gates(0)
            sp.wait_ge(w_ready, NPARTS)
            load_aw(0)
            spill_xn(3)
            sp.dma_start(rope[:], rope_tab).then_inc(rope_in, 16)

            store_gates(1)
            with sp.Fori(2, NB) as tb:
                store_gates(tb)

            sp.wait_ge(down_d, NB * MT)
            sp.wait_ge(gate_out, 16 * KT * NB)
            load_decay(0)
            sp.wait_ge(aw_lo, PT)
            sp.dma_start(stage[:, 0:HG, :], out_w[0]).then_inc(ow_in, 16)
            sp.wait_ge(xn_out, 16 * NB)

            def load_xn(n, b):
                sp.wait_ge(proj_d, n * PT + PT)
                sp.dma_start(xn0[:].bitcast(F32), xn_dram[b]).then_inc(xn_in, 16)

            def load_fin(b, u):
                sp.dma_start(fin_in[:, u % FINR, 0, :], x_t[u, :, bass.ts(b, S)]).then_inc(fin_ld[u % FINR], 16)
                sp.dma_start(fin_in[:, u % FINR, 1, :], g_dram[u, :, bass.ts(b, S)]).then_inc(fin_ld[u % FINR], 16)

            def group(g, final):
                for b in range(NB):
                    n = g * NB + b
                    if b == NB - 1 and not final:
                        sp.wait_ge(decayed, n * NDEC + NDEC)
                        load_decay(g + 1)
                    if final:
                        if b == 0:
                            sp.wait_ge(ow_lo, g * HG + HG)
                        for u in range(FINR):
                            load_fin(b, u)
                    if b == 0 and not final:
                        sp.wait_ge(ow_lo, g * HG + HG)
                        sp.dma_start(stage[:], attn_w[g + 1]).then_inc(aw_in, 16)
                    if b == NB - 1 and not final:
                        sp.wait_ge(aw_lo, g * PT + 2 * PT)
                        sp.dma_start(stage[:, 0:HG, :], out_w[g + 1]).then_inc(ow_in, 16)
                    if not (final and b >= NB - 2):
                        load_xn(n + 1, (b + 2) % NB)
                    if final:
                        for u in range(KT):
                            sp.wait_ge(fin_d, b * KT + u + 1)
                            sp.dma_start(out[u, :, bass.ts(b, S)], fin[:, u % 2, :]).then_inc(stored[u % 2], 16)
                            if u + FINR < KT:
                                load_fin(b, u + FINR)

            load_xn(0, 1)
            with sp.Fori(0, NG - 1) as g:
                group(g, False)
            group(NG - 1, True)
            for parity in range(2):
                sp.wait_ge(stored[parity], 8 * KT * NB)

        @block.scalar
        def _(act):
            def norm(i):
                tb, j = divmod(i, TT)
                act.wait_ge(rstd_d, tb + 1)
                act.activation(x_sb[:, tb % 2, j, :], x_sb[:, tb % 2, j, :], ACT.Identity,
                               bias=nmr[:, tb, j:j + 1], scale=rstd[:, tb, j:j + 1]).then_inc(normed, 1)

            def norm_hi(i):
                tb, j = divmod(i, TT)
                act.wait_ge(ln_t, i + 1)
                dst = xn0[:, 0, :, bass.ts(j, P)] if tb == 0 else xn123[:, tb - 1, 0, :, bass.ts(j, P)]
                act.copy(dst, ln_ps(i)[:].rearrange("p (k c) -> p k c", k=KT)).then_inc(ln_hi, 1)

            def silu_gate(tb, m):
                act.wait_ge(gu_done, tb * (2 * MT) + 2 * m + 1)
                if m >= 2 or not (isinstance(tb, int) and tb == 0):
                    act.wait_ge(f_lo, tb * MT + m - 1)
                act.activation(fz[:, m % 2, :], gu_ps[(2 * m) % 3][:], ACT.Silu,
                               scale=scale_sb[:, m:m + 1]).then_inc(silu_d, 1)

            def fuse_hi(tb, m):
                act.wait_ge(f_d, tb * MT + m + 1)
                if m >= FRING or not (isinstance(tb, int) and tb == 0):
                    act.wait_ge(down_d, tb * MT + m - FRING + 1)
                act.copy(fsplit[:, m % FRING, 0, :], fz[:, m % 2, :]).then_inc(f_hi, 1)

            def gates(tb):
                act.wait_ge(down_d, tb * MT + MT)
                if not (isinstance(tb, int) and tb == 0):
                    act.wait_ge(gate_out, tb * (16 * KT))
                for d in range(KT):
                    act.activation(gout[:, d, :], down_ps[d][:], ACT.Silu,
                                   scale=scale_sb[:, 2 * MT + d:2 * MT + d + 1]).then_inc(gate_d, 1)

            def aw_split_hi(g, t):
                act.wait_ge(aw_in, g * 16 + 16)
                act.copy(aw[:, 0, t, :, :], stage[:, t, :]).then_inc(aw_hi, 1)

            for i in range(TT):
                norm(i)
            for i in range(TT):
                norm_hi(i)
            act.wait_ge(const_in, 16)
            for tb in range(2):
                for m in range(MT):
                    tile = LN_AT.get((tb, m))
                    silu_gate(tb, m)
                    if tile is not None:
                        norm(tile)
                    fuse_hi(tb, m)
                    if tile is not None:
                        norm_hi(tile)
                    if tb >= 1 and m == FLAG - 1:
                        gates(tb - 1)
                    for t in AW_AT.get((tb, m), ()):
                        aw_split_hi(0, t)

            def ow_split_hi(g, h):
                act.wait_ge(ow_in, g * 16 + 16)
                if h == 0:
                    if_later(act, g, lambda: act.wait_ge(out_d, g * (NB * KT)))
                act.copy(ow[:, 0, h, :], stage[:, h, :]).then_inc(ow_hi, 1)

            with act.Fori(2, NB) as tb:
                for m in range(MT):
                    silu_gate(tb, m)
                    fuse_hi(tb, m)
                    if m == FLAG - 1:
                        gates(tb - 1)
            act.wait_ge(down_d, NB * MT)
            act.wait_ge(xn_out, 16 * NB)

            def qk_round(n, r):
                first = isinstance(n, int) and n == 0
                act.wait_ge(qk_sum, n * QK + r + 1)
                if not first:
                    act.wait_ge(score_d, n * NBL)
                dst = k_r[:, 0, :] if r == 0 else q_r[:, 0, r - 1, :]
                act.copy(dst, rot1[:, r % RRING, :]).then_inc(qk_hi, 1)

            def turn(n, r):
                first = isinstance(n, int) and n == 0
                tile = 0 if r == 0 else r + 1
                ps = proj_bank(n, tile)
                act.wait_ge(proj_d, n * PT + tile + 1)
                if r >= RRING:
                    act.wait_ge(qk_sum, n * QK + r - RRING + 1)
                elif r == 0 and not first:
                    act.wait_ge(qk_sum, n * QK)
                act.copy(rot2[0:ROT, r % RRING, :], ps[ROT:, :])
                act.copy(rot2[ROT:, r % RRING, :], ps[0:ROT, :]).then_inc(turned, 1)

            def copy_vt(n):
                act.wait_ge(proj_d, n * PT + 2)
                if not (isinstance(n, int) and n == 0):
                    act.wait_ge(vt_d, n)
                act.copy(vt_sb[:], proj_bank(n, 1)[:]).then_inc(vt_copied, 1)

            def v_round(n):
                act.wait_ge(vt_d, n + 1)
                if not (isinstance(n, int) and n == 0):
                    act.wait_ge(d_used, n * NEL)
                act.copy(v_r[:, 0, :, :], vt_bank(n)[:].rearrange("p (t e) -> p t e", t=TT)).then_inc(v_hi, 1)

            def kn_round(n):
                act.wait_ge(kt_d, n + 1)
                act.copy(kn_r[:, 0, :, :], kt_bank(n)[:, 0:HALF].rearrange("p (t e) -> p t e", t=VD)).then_inc(kn_hi, 1)

            def st_round(n):
                act.wait_ge(d_used, n * NEL + VD)
                if isinstance(n, int) and n == 0:
                    act.wait_ge(gate_out, 16 * KT * NB)
                act.copy(st_r[:, 0, :, :], st_ps[:].rearrange("p (h e) -> p h e", h=HG)).then_inc(st_hi, 1)

            def decayed_round(n, e):
                if VD <= e < SC:
                    act.wait_ge(q_decayed, n * HG + 2 * (e - VD) + 2)
                else:
                    act.wait_ge(decayed, n * NDEC + (e if e < VD else e - QD) + 1)
                if e >= SRING:
                    act.wait_ge(d_used, n * NEL + e - SRING + 1)
                else:
                    if_later(act, n, lambda: act.wait_ge(d_used, n * NEL + (e - SRING + 1)))
                act.copy(d_r[:, e % SRING, 0, :], d_sb[:, e % SRING, :]).then_inc(d_hi, 1)

            def projections(n, beside={}):
                for other in beside.get(0, ()):
                    other()
                copy_vt(n)
                for r in range(1, QK):
                    for other in beside.get(r, ()):
                        other()
                    turn(n, r)
                    qk_round(n, r - 1)
                    if r == 1:
                        v_round(n)
                        kn_round(n)
                    if r == 2:
                        for e in range(VD):
                            decayed_round(n, e)
                decayed_round(n, VD)
                qk_round(n, QK - 1)
                decayed_round(n, VD + 1)
                st_round(n)

            def o_round(n, i):
                act.wait_ge(d_used, n * NEL + SC + ODONE[i] + 1)
                if not (isinstance(n, int) and n == 0) and i == 0:
                    act.wait_ge(out_d, n * KT)
                hs, qs = OTILES[i]
                act.copy(o_r[:, 0, hs, qs], o_ps[i][:].rearrange("p (h c) -> p h c", h=hs.stop - hs.start)).then_inc(o_hi, 1)

            def step(n, g, b, start=False, edge=False, final=False, last=False):
                for t in range(HEAD, NBL):
                    decayed_round(n, SC + t)
                if edge:
                    aw_split_hi(g + 1, 0)
                for i in range(2):
                    o_round(n, i)
                if edge:
                    aw_split_hi(g + 1, 1)
                elif not last:
                    turn(n + 1, 0)
                for i in range(2, NOT):
                    o_round(n, i)
                if edge:
                    aw_split_hi(g + 1, 2)
                    turn(n + 1, 0)
                if last:
                    return
                beside = {}
                if edge:
                    beside = {r: [lambda t=t: aw_split_hi(g + 1, t) for t in ts] for r, ts in ((0, (3, 4)), (1, (5,)))}
                if start:
                    beside = {r: [lambda h=h: ow_split_hi(g, h) for h in hs] for r, hs in ((0, (0, 1, 2)), (1, (3,)))}
                projections(n + 1, beside)
                for t in range(HEAD):
                    decayed_round(n + 1, SC + t)

            turn(0, 0)
            gates(NB - 1)
            projections(0)
            for t in range(HEAD):
                decayed_round(0, SC + t)
            run_steps(act, step)

        @block.vector
        def _(dve):
            def mean_var(tb):
                if tb >= 1:
                    dve.wait_ge(x_in[tb % 2], 16 * ((tb + 1) // 2))
                if tb >= 1:
                    dve.wait_ge(rstd_d, tb)
                for j in range(TT):
                    if tb == 0:
                        dve.wait_ge(x0_in[j], 16)
                    dve.bn_stats(stats[:, j, :], x_sb[:, tb % 2, j, :]).then_inc(stats_d, 1)
                dve.wait_ge(stats_d, TT * (tb + 1))
                for j in range(TT):
                    dve.bn_aggr(mv[:, j, :], stats[:, j, :]).then_inc(newton, 1)
                dve.wait_ge(newton, 9 * tb + 4)
                dve.tensor_scalar(rs[:, 0, :], mv[:, :, 1], EPS, None, ALU.add).then_inc(var_d, 1)

            def inv_std(tb):
                dve.wait_ge(pow_d, tb + 1)
                c = 9 * tb + 4
                dve.tensor_tensor(rs[:, 3, :], rs[:, 2, :], rs[:, 2, :], ALU.mult).then_inc(newton, 1)
                dve.wait_ge(newton, c + 1)
                dve.tensor_tensor(rs[:, 4, :], rs[:, 3, :], rs[:, 0, :], ALU.mult).then_inc(newton, 1)
                dve.wait_ge(newton, c + 2)
                dve.tensor_scalar(rs[:, 5, :], rs[:, 4, :], -0.5, 1.5, ALU.mult, ALU.add).then_inc(newton, 1)
                dve.wait_ge(newton, c + 3)
                dve.tensor_tensor(rstd[:, tb, :], rs[:, 5, :], rs[:, 2, :], ALU.mult).then_inc(newton, 1)
                dve.wait_ge(newton, c + 4)
                dve.tensor_tensor(rs[:, 3, :], mv[:, :, 0], rstd[:, tb, :], ALU.mult).then_inc(newton, 1)
                dve.wait_ge(newton, c + 5)
                dve.tensor_scalar(nmr[:, tb, :], rs[:, 3, :], -1.0, None, ALU.mult).then_inc(rstd_d, 1)

            def norm_lo(i):
                tb, j = divmod(i, TT)
                dve.wait_ge(ln_hi, i + 1)
                parts = xn0 if tb == 0 else xn123[:, tb - 1]
                hi = parts[:, 0, :, bass.ts(j, P)]
                lo = parts[:, 1, :, bass.ts(j, P)]
                dve.tensor_tensor(lo, ln_ps(i)[:].rearrange("p (k c) -> p k c", k=KT), hi.bitcast(F32),
                                  ALU.subtract).then_inc(ln_lo, 1)

            def w_exponent(q):
                dve.wait_ge(w_in[q % WRING], 16 * (q // WRING + 1))
                if q >= MRING:
                    dve.wait_ge(w_ready, q - MRING + 1)
                dve.tensor_scalar(magic[:, q % MRING, :].bitcast(I32), stage[:, q % WRING, :].bitcast(I32),
                                  EXP_MASK, None, ALU.bitwise_and).then_inc(k_exp, 1)

            def w_magic(q):
                dve.wait_ge(k_exp, q + 1)
                dve.tensor_scalar(magic[:, q % MRING, :], magic[:, q % MRING, :], F8_SCALE, F8_FLOOR,
                                  ALU.mult, ALU.max).then_inc(k_made, 1)

            def w_round(q):
                dve.wait_ge(k_added, q + 1)
                dve.tensor_tensor(gu_w[:, q // PARTS, q % PARTS, :, :],
                                  stage[:, q % WRING, :].rearrange("p (k c) -> p k c", k=KT),
                                  magic[:, q % MRING, :].rearrange("p (k c) -> p k c", k=KT),
                                  ALU.subtract).then_inc(w_ready, 1)

            def fuse(tb, m):
                dve.wait_ge(gu_done, tb * (2 * MT) + 2 * m + 2)
                dve.wait_ge(silu_d, tb * MT + m + 1)
                dve.scalar_tensor_tensor(out=fz[:, m % 2, :], in0=gu_ps[(2 * m + 1) % 3][:],
                                         scalar=scale_sb[:, MT + m:MT + m + 1], in1=fz[:, m % 2, :],
                                         op0=ALU.mult, op1=ALU.mult).then_inc(f_d, 1)

            def aw_split_lo(g, t):
                dve.wait_ge(aw_hi, g * PT + t + 1)
                dve.tensor_tensor(aw[:, 1, t, :, :],
                                  stage[:, t, :].rearrange("p (k c) -> p k c", k=KT),
                                  aw[:, 0, t, :, :].bitcast(F32), ALU.subtract).then_inc(aw_lo, 1)

            mean_var(0)
            inv_std(0)

            def w_step(q):
                if q + MLEAD < NPARTS:
                    w_exponent(q + MLEAD)
                w_round(q)
                if q + MLEAD < NPARTS:
                    w_magic(q + MLEAD)

            for q in range(MLEAD):
                w_exponent(q)
            for q in range(MLEAD):
                w_magic(q)
            w_step(0)
            for i in range(TT):
                norm_lo(i)
            for q in range(1, PARTS):
                w_step(q)
            dve.wait_ge(const_in, 16)
            for tb in range(2):
                for m in range(MT):
                    if tb == 0 and m + 1 < MT:
                        for q in range(PARTS * (m + 1), PARTS * (m + 2)):
                            w_step(q)
                    if (tb, m) == (0, 3):
                        inv_std(1)
                    fuse(tb, m)
                    if (tb, m) == (0, 2):
                        mean_var(1)
                    if (tb, m) in LN_AT:
                        norm_lo(LN_AT[tb, m])
                    if (tb, m) in ((0, 11), (1, 2)):
                        mean_var(2 + tb)
                    if (tb, m) in ((1, 0), (1, 3)):
                        inv_std(2 + m // 3)
                    for t in AW_AT.get((tb, m), ()):
                        aw_split_lo(0, t)

            def ow_split_lo(g, h):
                dve.wait_ge(ow_hi, g * HG + h + 1)
                dve.tensor_tensor(ow[:, 1, h, :], stage[:, h, :], ow[:, 0, h, :].bitcast(F32),
                                  ALU.subtract).then_inc(ow_lo, 1)

            with dve.Fori(2, NB) as tb:
                for m in range(MT):
                    fuse(tb, m)
            dve.wait_ge(down_d, NB * MT)
            dve.wait_ge(xn_out, 16 * NB)
            dve.wait_ge(rope_in, 16)
            dve.wait_ge(k_decay_in, 16)

            def rotate(n, r):
                first = isinstance(n, int) and n == 0
                tile = 0 if r == 0 else r + 1
                dve.wait_ge(turned, n * QK + r + 1)
                if r >= RRING:
                    dve.wait_ge(qk_lo, n * QK + r - RRING + 1)
                    if r == RRING:
                        dve.wait_ge(kt_d, n + 1)
                    else:
                        dve.wait_ge(q_decayed, n * HG + r - RRING)
                elif r == 0 and not first:
                    dve.wait_ge(qk_lo, n * QK)
                    dve.wait_ge(q_decayed, n * HG)
                dve.tensor_tensor(rot1[:, r % RRING, :], proj_bank(n, tile)[:], rope[:, 0, :], ALU.mult)
                dve.tensor_tensor(rot2[:, r % RRING, :], rot2[:, r % RRING, :], rope[:, 1, :],
                                  ALU.mult).then_inc(rot_d, 1)

            def qk_rest(n, r):
                dve.wait_ge(qk_hi, n * QK + r + 1)
                dst, hi = (k_r[:, 1, :], k_r[:, 0, :]) if r == 0 else (q_r[:, 1, r - 1, :], q_r[:, 0, r - 1, :])
                dve.tensor_tensor(dst, rot1[:, r % RRING, :], hi.bitcast(F32), ALU.subtract).then_inc(qk_lo, 1)

            def v_rest(n):
                dve.wait_ge(v_hi, n + 1)
                dve.tensor_tensor(v_r[:, 1, :, :], vt_bank(n)[:].rearrange("p (t e) -> p t e", t=TT),
                                  v_r[:, 0, :, :].bitcast(F32), ALU.subtract).then_inc(v_lo, 1)

            def v_decay(n, g, j):
                if_later(dve, n, lambda: dve.wait_ge(d_lo, n * NEL + (j - SRING + 1)))
                dve.tensor_tensor(d_sb[:, j, :].rearrange("p (h e) -> p h e", h=HG),
                                  vt_bank(n)[:, bass.ts(j, P)].unsqueeze(1).broadcast_to([P, HG, DH]),
                                  k_decay[:, g, j, :].unsqueeze(2).broadcast_to([P, HG, DH]), ALU.mult).then_inc(decayed, 1)

            def q_decay_head(n, h):
                e = VD + h // 2
                if h % 2 == 0:
                    if_later(dve, n, lambda: dve.wait_ge(d_lo, n * NEL + (e - SRING + 1)))
                dve.tensor_tensor(d_sb[:, e, bass.ts(h % 2, HALF)], rot1[:, (h + 1) % RRING, HALF:S],
                                  q_decay[:, h, :], ALU.mult).then_inc(q_decayed, 1)

            def kn_rest(n):
                dve.wait_ge(kn_hi, n + 1)
                dve.tensor_tensor(kn_r[:, 1, :, :], kt_bank(n)[:, 0:HALF].rearrange("p (t e) -> p t e", t=VD),
                                  kn_r[:, 0, :, :].bitcast(F32), ALU.subtract).then_inc(kn_lo, 1)

            def st_rest(n):
                dve.wait_ge(st_hi, n + 1)
                dve.tensor_tensor(st_r[:, 1, :, :], st_ps[:].rearrange("p (h e) -> p h e", h=HG),
                                  st_r[:, 0, :, :].bitcast(F32), ALU.subtract).then_inc(st_lo, 1)

            def projections(n, g, tables=None, beside={}):
                for other in beside.get(0, ()):
                    other()
                for r in range(1, QK):
                    for other in beside.get(r, ()):
                        other()
                    rotate(n, r)
                    qk_rest(n, r - 1)
                    if r == 1:
                        v_rest(n)
                        for j in range(VD):
                            v_decay(n, g, j)
                        kn_rest(n)
                    if r == 2 and tables is not None:
                        dve.wait_ge(decay_in, tables * 32 + 32)
                    if r >= 2:
                        q_decay_head(n, r - 2)
                qk_rest(n, QK - 1)
                q_decay_head(n, HG - 1)

            def decay_block(n, t):
                j, h0, nh, i0, ni = BLOCKS[t]
                e = SC + t
                dve.wait_ge(score_d, n * NBL + t + 1)
                if e >= SRING:
                    dve.wait_ge(d_lo, n * NEL + e - SRING + 1)
                else:
                    if_later(dve, n, lambda: dve.wait_ge(d_lo, n * NEL + (e - SRING + 1)))
                by_head = lambda ap: ap.rearrange("p (h i c) -> p h i c", h=nh, i=ni)
                dve.tensor_tensor(by_head(d_sb[:, e % SRING, :]), by_head(sc_ps[t % TRING][:]),
                                  decay[:, h0:h0 + nh, i0 - j:i0 - j + ni, :], ALU.mult).then_inc(decayed, 1)

            def o_rest(n, i):
                dve.wait_ge(o_hi, n * NOT + i + 1)
                hs, qs = OTILES[i]
                dve.tensor_tensor(o_r[:, 1, hs, qs], o_ps[i][:].rearrange("p (h c) -> p h c", h=hs.stop - hs.start),
                                  o_r[:, 0, hs, qs].bitcast(F32), ALU.subtract).then_inc(o_lo, 1)

            def accumulate(n, b, u):
                dve.wait_ge(out_d, n * KT + u + 1)
                dve.tensor_tensor(acc[:, b, u, :], out_ps[u][:], acc[:, b, u, :], ALU.add).then_inc(acc_d, 1)

            def finish(n, b, u):
                accumulate(n, b, u)
                dve.wait_ge(acc_d, n * KT + KT + u + 1)
                loads = len(range(u % FINR, KT, FINR))
                dve.wait_ge(fin_ld[u % FINR], b * (32 * loads) + (u // FINR + 1) * 32)
                dve.tensor_tensor(fin_in[:, u % FINR, 1, :], acc[:, b, u, :], fin_in[:, u % FINR, 1, :],
                                  ALU.mult).then_inc(fin_p, 1)
                dve.wait_ge(fin_p, b * KT + u + 1)
                if u >= 2:
                    dve.wait_ge(stored[u % 2], (b * (KT // 2) + u // 2) * 16)
                else:
                    if_later(dve, b, lambda: dve.wait_ge(stored[u % 2], b * (KT // 2) * 16))
                dve.tensor_tensor(fin[:, u % 2, :], fin_in[:, u % FINR, 1, :], fin_in[:, u % FINR, 0, :],
                                  ALU.add).then_inc(fin_d, 1)

            def step(n, g, b, start=False, edge=False, final=False, last=False):
                for t in range(HEAD, NBL):
                    decay_block(n, t)
                if edge:
                    aw_split_lo(g + 1, 0)
                for i in range(2):
                    o_rest(n, i)
                if edge:
                    aw_split_lo(g + 1, 1)
                elif not last:
                    rotate(n + 1, 0)
                for i in range(2, NOT):
                    o_rest(n, i)
                if edge:
                    aw_split_lo(g + 1, 2)
                    rotate(n + 1, 0)
                if not last:
                    beside = {}
                    if edge:
                        beside = {r: [lambda t=t: aw_split_lo(g + 1, t) for t in ts] for r, ts in ((0, (3, 4)), (1, (5,)))}
                    if start:
                        beside = {r: [lambda h=h: ow_split_lo(g, h) for h in hs] for r, hs in ((0, (0, 1, 2)), (1, (3,)))}
                    projections(n + 1, g + 1 if edge else g, g + 1 if edge else None, beside)
                for u in range(KT):
                    if u == 2 and not last:
                        st_rest(n + 1)
                    if u == KT - 1 and not last:
                        for t in range(HEAD):
                            decay_block(n + 1, t)
                    if final:
                        finish(n, b, u)
                    else:
                        accumulate(n, b, u)

            rotate(0, 0)
            projections(0, 0, 0)
            st_rest(0)
            for t in range(HEAD):
                decay_block(0, t)
            dve.wait_ge(zeroed, NB)
            dve.sem_inc(acc_d, KT)
            run_steps(dve, step)

        @block.gpsimd
        def _(pool):
            pool.memset(rs[:, 1, :], -0.5).then_inc(pow_c, 1)
            pool.wait_ge(pow_c, 1)

            def power(tb):
                pool.wait_ge(var_d, tb + 1)
                if tb >= 1:
                    pool.wait_ge(rstd_d, tb)
                pool.tensor_tensor(rs[:, 2, :], rs[:, 0, :], rs[:, 1, :], ALU.pow).then_inc(pow_d, 1)

            def w_add(q):
                pool.wait_ge(k_made, q + 1)
                pool.tensor_tensor(stage[:, q % WRING, :], stage[:, q % WRING, :], magic[:, q % MRING, :],
                                   ALU.add).then_inc(k_added, 1)

            def fuse_rest(tb, m):
                pool.wait_ge(f_hi, tb * MT + m + 1)
                pool.tensor_tensor(fsplit[:, m % FRING, 1, :], fz[:, m % 2, :], fsplit[:, m % FRING, 0, :].bitcast(F32),
                                   ALU.subtract).then_inc(f_lo, 1)

            power(0)
            for q in range(PARTS + MLEAD):
                w_add(q)
            for tb in range(2):
                for m in range(MT):
                    if (tb, m) == (0, 3):
                        power(1)
                    if tb == 0:
                        for q in range(PARTS * (m + 1) + MLEAD, min(PARTS * (m + 2) + MLEAD, NPARTS)):
                            w_add(q)
                    if (tb, m) in ((1, 0), (1, 3)):
                        power(2 + m // 3)
                    fuse_rest(tb, m)
            with pool.Fori(2, NB) as tb:
                for m in range(MT):
                    fuse_rest(tb, m)

            pool.wait_ge(down_d, NB * MT)

            def zero(b):
                pool.memset(acc[:, b], 0.0).then_inc(zeroed, 1)

            def decayed_rest(n, e):
                pool.wait_ge(d_hi, n * NEL + e + 1)
                pool.tensor_tensor(d_r[:, e % SRING, 1, :], d_sb[:, e % SRING, :],
                                   d_r[:, e % SRING, 0, :].bitcast(F32), ALU.subtract).then_inc(d_lo, 1)

            def projections(n, beside={}):
                for r in range(QK):
                    for other in beside.get(r, ()):
                        other()
                    pool.wait_ge(rot_d, n * QK + r + 1)
                    pool.tensor_tensor(rot1[:, r % RRING, :], rot1[:, r % RRING, :], rot2[:, r % RRING, :],
                                       ALU.add).then_inc(qk_sum, 1)
                    if r == 2:
                        for e in range(VD):
                            decayed_rest(n, e)
                for e in range(VD, SC):
                    decayed_rest(n, e)

            def step(n, g, b, start=False, edge=False, final=False, last=False):
                for t in range(HEAD, NBL):
                    decayed_rest(n, SC + t)
                if last:
                    return
                projections(n + 1)
                for t in range(HEAD):
                    decayed_rest(n + 1, SC + t)

            projections(0, {r: [lambda b=b: zero(b) for b in bs] for r, bs in ((0, (0, 1)), (1, (2,)), (2, (3,)))})
            for t in range(HEAD):
                decayed_rest(0, SC + t)
            run_steps(pool, step)

        @block.tensor
        def _(pe):
            def products(dst, pairs, start=True, stop=True):
                for x, (a, b) in enumerate(pairs):
                    last = pe.matmul(dst, a, b, start=start and x == 0, stop=stop and x == len(pairs) - 1)
                return last

            def ln_transpose(i):
                pe.wait_ge(normed, i + 1)
                if i > TT:
                    pe.wait_ge(ln_lo, i)
                for k in range(KT):
                    last = pe.transpose(ln_ps(i)[:, bass.ts(k, P)], x_sb[:, i // TT % 2, i % TT, bass.ts(k, P)], ident[:])
                last.then_inc(ln_t, 1)

            def gate_up(tb, m, s):
                q = 2 * m + s
                first = isinstance(tb, int) and tb == 0
                if not first or q >= 3:
                    was = q - 3
                    pe.wait_ge(f_d if was % 2 else silu_d, tb * MT + was // 2 + 1)
                for part in range(2):
                    if first and q == 0 and part == 1:
                        pe.wait_ge(ln_lo, TT)
                    last = products(gu_ps[q % 3][:], [(gu_w[:, m, s, k, :], xn_tb(tb, part, k)) for k in range(KT)],
                                    start=(part == 0), stop=(part == 1))
                last.then_inc(gu_done, 1)

            def down(tb, m):
                pe.wait_ge(f_lo, tb * MT + m + 1)
                if isinstance(tb, int) and tb == 0:
                    pe.wait_ge(w_ready, PARTS * (m + 1))
                if m == 0 and isinstance(tb, int) and tb == 0:
                    pe.wait_ge(ln_lo, TT)
                elif m == 0:
                    pe.wait_ge(gate_d, tb * KT)
                for d in range(KT):
                    last = products(down_ps[d][:], [(gu_w[:, m, 2, d, :], fsplit[:, m % FRING, part, :]) for part in range(2)],
                                    start=(m == 0), stop=(m == MT - 1))
                last.then_inc(down_d, 1)

            pe.wait_ge(ident_sem, 16)
            for i in range(TT):
                ln_transpose(i)
            pe.wait_ge(ln_hi, TT)
            for tb in range(2):
                if tb == 1:
                    pe.wait_ge(ln_lo, 2 * TT)
                for m in range(MT):
                    for part in range(2):
                        if tb == 0:
                            pe.wait_ge(w_ready, PARTS * m + part + 1)
                        gate_up(tb, m, part)
                    if (tb, m) in LN_AT:
                        ln_transpose(LN_AT[tb, m])
                    if m >= FLAG:
                        down(tb, m - FLAG)
                    elif tb >= 1:
                        down(tb - 1, m - FLAG + MT)
            pe.wait_ge(ln_lo, NB * TT)
            with pe.Fori(2, NB) as tb:
                for m in range(MT):
                    gate_up(tb, m, 0)
                    gate_up(tb, m, 1)
                    if m >= FLAG:
                        down(tb, m - FLAG)
                    else:
                        down(tb - 1, m - FLAG + MT)

            SPLIT = [(0, 0), (0, 1), (1, 0)]

            def project(n, tile, g_edge=None):
                first = isinstance(n, int) and n == 0
                if g_edge is not None:
                    pe.wait_ge(aw_lo, g_edge * PT + tile + 1)
                if tile == 0 and not first:
                    pe.wait_ge(xn_in, n * 16)
                if tile < 2 and not first:
                    pe.wait_ge(acc_d, (n - 1) * KT + 3 + tile)
                elif 2 <= tile < PT - 1 and not first:
                    pe.wait_ge(decayed, n * NDEC)
                elif tile == PT - 1 and not first:
                    pe.wait_ge(rot_d, n * QK + 1)
                products(proj_bank(n, tile)[:], [(aw[:, a, tile, k, :], xn0[:, c, k, :])
                                            for a, c in SPLIT for k in range(KT)]).then_inc(proj_d, 1)

            def transpose_v(n):
                pe.wait_ge(vt_copied, n + 1)
                if not (isinstance(n, int) and n == 0):
                    pe.wait_ge(o_lo, (n - 1) * NOT + 2)
                for j in range(TT):
                    last = pe.transpose(vt_bank(n)[:, bass.ts(j, P)], vt_sb[:, bass.ts(j, P)], ident[:])
                last.then_inc(vt_d, 1)

            def transpose_k(n):
                pe.wait_ge(qk_sum, n * QK + 1)
                if not (isinstance(n, int) and n == 0):
                    pe.wait_ge(o_lo, (n - 1) * NOT + 3)
                for j in range(VD):
                    last = pe.transpose(kt_bank(n)[:, bass.ts(j, P)], rot1[:, 0, bass.ts(j, P)], ident[:])
                last.then_inc(kt_d, 1)

            def state(n):
                pe.wait_ge(kn_lo, n + 1)
                if_later(pe, n, lambda: pe.wait_ge(o_lo, n * NOT))
                for j in range(VD):
                    pe.wait_ge(d_lo, n * NEL + j + 1)
                    products(st_ps[:], [(kn_r[:, a, j, :], d_r[:, j, c, :]) for a, c in SPLIT],
                                    start=(j == 0), stop=(j == VD - 1)).then_inc(d_used, 1)

            def inter(n):
                pe.wait_ge(st_lo, n + 1)
                pe.wait_ge(decayed, n * NDEC + VD)
                for x in range(QD):
                    pe.wait_ge(d_lo, n * NEL + VD + x + 1)
                    tile = inter_ps[x][:].rearrange("p (h c) -> p h c", h=2)
                    for h in range(2):
                        last = products(tile[:, h, :], [(st_r[:, a, 2 * x + h, :], d_r[:, VD + x, c, bass.ts(h, HALF)])
                                                        for a, c in SPLIT], start=(h == 0), stop=False)
                    last.then_inc(d_used, 1)

            def projections(n, g_edge=None, skip_first=1):
                for tile in range(skip_first, PT):
                    project(n, tile, g_edge)
                    if tile == 2:
                        transpose_v(n)
                        transpose_k(n)

            def scores(n, t):
                j, h0, nh, i0, ni = BLOCKS[t]
                if t >= TRING:
                    pe.wait_ge(decayed, n * NDEC + VD + t - TRING + 1)
                elif t == 0:
                    pe.wait_ge(qk_lo, n * QK + QK)
                    if_later(pe, n, lambda: pe.wait_ge(acc_d, n * KT + 2))
                products(sc_ps[t % TRING][:], [(k_r[:, a, bass.ts(j, P)], q_r[:, c, h0:h0 + nh, i0 * P:(i0 + ni) * P])
                                               for a, c in SPLIT]).then_inc(score_d, 1)

            def times_v(n, t):
                j, h0, nh, i0, ni = BLOCKS[t]
                e = SC + t
                pairs = lambda cols: [(v_r[:, a, j, :], d_r[:, e % SRING, c, cols]) for a, c in SPLIT]
                if t == 0:
                    pe.wait_ge(v_lo, n + 1)
                if t == NBL - 1:
                    pe.wait_ge(o_lo, n * NOT + 1)
                pe.wait_ge(d_lo, n * NEL + e + 1)
                if t == 0:
                    for x in range(2):
                        tile = o_ps[x][:].rearrange("p (h c) -> p h c", h=2)[:, :, P:HALF]
                        last = products(tile, pairs(slice(x * HALF, (x + 1) * HALF)), start=False, stop=False)
                    last.then_inc(d_used, 1)
                else:
                    x = OF_BLOCK[t]
                    products(o_ps[x][:], pairs(slice(0, S)), start=t in (3, 5), stop=t in ODONE).then_inc(d_used, 1)

            def out_projection(n, g, u, last):
                if u == 0:
                    pe.wait_ge(acc_d, n * KT + KT) if last else pe.wait_ge(vt_copied, n + 2)
                elif u == 1:
                    if not last:
                        pe.wait_ge(rot_d, n * QK + QK + 2)
                elif u == 2:
                    if not last:
                        pe.wait_ge(rot_d, n * QK + 2 * QK)
                else:
                    pe.wait_ge(acc_d, n * KT + KT + 1)
                products(out_ps[u][:], [(ow[:, a, h, bass.ts(u, P)], o_r[:, c, h, :])
                                        for h in range(HG) for a, c in SPLIT]).then_inc(out_d, 1)

            def step(n, g, b, start=False, edge=False, final=False, last=False):
                g_edge = g + 1 if edge else None
                for t in range(HEAD, NBL + LAG):
                    if t < NBL:
                        scores(n, t)
                    if t == (NBL + 2 if edge else NBL) and not last:
                        project(n + 1, 0, g_edge)
                    if t >= LAG:
                        times_v(n, t - LAG)
                if not last:
                    projections(n + 1, g_edge)
                pe.wait_ge(o_lo, n * NOT + NOT)
                if start:
                    pe.wait_ge(ow_lo, g * HG + HG)
                for u in range(KT):
                    if u == 2 and not last:
                        state(n + 1)
                    if u == KT - 1 and not last:
                        for t in range(HEAD):
                            scores(n + 1, t)
                        inter(n + 1)
                    out_projection(n, g, u, last)

            pe.wait_ge(f_d, NB * MT - 1)
            down(NB - 1, MT - 2)
            project(0, 0, 0)
            down(NB - 1, MT - 1)
            pe.wait_ge(silu_d, NB * MT)
            pe.wait_ge(f_d, NB * MT)
            project(0, 1, 0)
            project(0, 2, 0)
            pe.wait_ge(gate_d, NB * KT)
            transpose_v(0)
            transpose_k(0)
            projections(0, 0, skip_first=3)
            state(0)
            for t in range(HEAD):
                scores(0, t)
            inter(0)
            run_steps(pe, step)


def if_later(eng, n, wait):
    if not isinstance(n, int) or n > 0:
        wait()


def _constants():
    import numpy as np
    f = np.float32
    inv = f(1.0) / np.power(f(10000.0), np.arange(0, DH, 2, dtype=f) / f(DH)).astype(f)
    angle = (np.arange(S, dtype=f)[:, None] * inv[None, :]).astype(f).T.astype(np.float64)
    cos, sin = np.cos(angle), np.sin(angle)
    rope = np.stack([np.concatenate([cos, cos]), np.concatenate([-sin, sin])], axis=1).astype(f)
    lam = np.exp2(-8.0 * np.arange(1, H + 1, dtype=np.float64) / H)
    j = np.arange(P)[:, None, None]
    dist = P * np.arange(2)[None, :, None] + np.arange(P)[None, None, :] - j
    table = np.where(dist >= 0, np.exp(-lam[:, None, None, None] * np.maximum(dist, 0)), 0.0)
    decay = table.reshape(NG, HG, P, 2, P).transpose(0, 2, 1, 3, 4).astype(f)
    q_decay = np.exp(-lam[:, None] * np.arange(1, HALF + 1)).reshape(NG, 1, HG, HALF)
    q_decay = np.broadcast_to(q_decay, (NG, P, HG, HALF)).astype(f)
    k_decay = np.exp(-lam[:, None] * np.arange(HALF - 1, -1, -1)).reshape(NG, HG, VD, P).transpose(3, 0, 2, 1).astype(f)
    c = np.ascontiguousarray
    return rope, c(decay), c(q_decay), c(k_decay), np.eye(P, dtype=f)


def kernel(L0_attn_x, L0_attn_wq, L0_attn_wk, L0_attn_wv, L0_attn_wo, L0_ffn_gate_w, L0_ffn_up_w, L0_ffn_down_w,
           L0_ffn_gate_scale, L0_ffn_up_scale, L0_ffn_down_scale):
    import numpy as np
    import concourse.bacc as bacc
    from concourse.bass_utils import run_bass_kernel_spmd

    c = np.ascontiguousarray
    x = np.asarray(L0_attn_x)
    x_nat = c(x.reshape(NB, TT, P, D).transpose(0, 2, 1, 3))
    x_t = c(x.reshape(NB * S, KT, P).transpose(1, 2, 0))
    wq = np.asarray(L0_attn_wq).reshape(NG, HG, DH, KT, P)
    wk = np.asarray(L0_attn_wk).reshape(NG, 1, DH, KT, P)
    wv = np.asarray(L0_attn_wv).reshape(NG, 1, DH, KT, P)
    attn_w = c(np.concatenate([wk, wv, wq], axis=1).transpose(0, 4, 1, 3, 2).reshape(NG, P, PT, KT * P))
    out_w = c(np.asarray(L0_attn_wo).reshape(D, NG, HG, P).transpose(1, 3, 2, 0))
    gu = [np.asarray(w).reshape(KT, P, MT, P).transpose(2, 1, 0, 3) for w in (L0_ffn_gate_w, L0_ffn_up_w)]
    dw = np.asarray(L0_ffn_down_w).reshape(MT, P, KT, P)
    mlp_w = c(np.stack(gu + [dw], axis=2).reshape(MT, P, PARTS, KT * P))
    scales = c(np.concatenate([np.asarray(L0_ffn_gate_scale).reshape(MT, P), np.asarray(L0_ffn_up_scale).reshape(MT, P),
                               np.asarray(L0_ffn_down_scale).reshape(KT, P)]).T)
    rope, decay, q_decay, k_decay, ident = _constants()
    arrays = {"x_nat": x_nat, "x_t": x_t, "attn_w": attn_w, "out_w": out_w, "mlp_w": mlp_w, "scales": scales,
              "rope": rope, "decay": decay, "q_decay": q_decay, "k_decay": k_decay, "ident": ident}

    nc = bacc.Bacc("TRN2", target_bir_lowering=False, num_devices=1)
    args = [nc.dram_tensor(f"in_{k}", a.shape, F32, kind="ExternalInput").ap() for k, a in arrays.items()]
    out = nc.dram_tensor("out_t", (KT, P, NB * S), F32, kind="ExternalOutput").ap()
    attention_mlp_kernel(nc, *args, out)
    r = run_bass_kernel_spmd(nc, [{f"in_{k}": a for k, a in arrays.items()}], core_ids=[0])
    got = r.results[0]["out_t"]
    return got.reshape(D, NB, S).transpose(1, 2, 0)
```

```python
from contextlib import ExitStack

import concourse.bass as bass
from concourse import mybir

F32 = mybir.dt.float32
F32R = mybir.dt.float32r
I32 = mybir.dt.int32
ALU = mybir.AluOpType
ACT = mybir.ActivationFunctionType

P = 128
NB, S, D = 4, 512, 512
H, HKV, DH = 16, 4, 128
FF = 1536
EPS = 1e-5
KT = D // P
TT = S // P
MT = FF // P
NG = HKV
HG = H // HKV
PT = 2 + HG
ROT = DH // 2
HALF = S // 2
BLOCKS = [(3, 0, HG, 3, 1), (2, 0, 2, 2, 2), (2, 2, 2, 2, 2), (0, 0, HG, 1, 1), (1, 0, HG, 1, 1), (0, 0, HG, 0, 1)]
NBL = len(BLOCKS)
OTILES = [(slice(0, 2), slice(HALF, S)), (slice(2, 4), slice(HALF, S)),
          (slice(0, HG), slice(P, 2 * P)), (slice(0, HG), slice(0, P))]
ODONE = [1, 2, 4, 5]
OF_BLOCK = [None, 0, 1, 2, 2, 3]
NOT = len(OTILES)
LAG = 3
VD = HALF // P
QD = HG // 2
SC = VD + QD
NEL = SC + NBL
NDEC = VD + NBL
SRING = 5
HEAD = 3
RRING = 3
FINR = 3
FLAG = 2
FRING = FLAG + 1
PARTS = 3
NPARTS = MT * PARTS
WRING = 6
MRING = 3
MLEAD = MRING - 1

LN_AT = {(0, m): TT + i for i, m in enumerate((5, 7, 9, 11))} | {(1, m): 2 * TT + m - 1 for m in range(1, 2 * TT + 1)}
AW_AT = {(1, m): (2 * (m - 8), 2 * (m - 8) + 1) for m in (8, 9, 10)}
TRING = 3
QK = 1 + HG

EXP_MASK = 0x7F800000
F8_SCALE = 1.5 * 2.0**20
F8_FLOOR = 1.5 * 2.0**14


def attention_mlp_kernel(nc, x_nat, x_t, attn_w, out_w, mlp_w, scales, rope_tab, decay_tab, q_decay_tab,
                         k_decay_tab, ident_in, out):
    ctx = ExitStack()
    with ctx:
        sem = lambda name: ctx.enter_context(nc.semaphore(name))

        def sb(name, shape, dt=F32, scope=ctx):
            return scope.enter_context(nc.sbuf_tensor(name, shape, dt))

        xn_dram = nc.dram_tensor("xn_split", (NB, P, 2, KT, S), F32, kind="Internal").ap()
        g_dram = nc.dram_tensor("mlp_gate", (KT, P, NB * S), F32, kind="Internal").ap()

        ident = sb("ident", [P, P])
        k_decay = sb("k_decay", [P, NG, VD, HG])
        xn0 = sb("xn0", [P, 2, KT, S], F32R)
        stage = sb("stage", [P, WRING, KT * P])
        early = ExitStack()
        x_sb = sb("x_sb", [P, 2, TT, D], scope=early)
        magic = sb("magic", [P, MRING, KT * P], scope=early)
        early_end = nc.sbuf_base
        early.close()
        aw = sb("aw", [P, 2, PT, KT, P], F32R)
        rope = sb("rope", [P, 2, S])
        assert nc.sbuf_base >= early_end

        mlp = ExitStack()
        xn123 = sb("xn123", [P, NB - 1, 2, KT, S], F32R, scope=mlp)
        gu_w = sb("gu_w", [P, MT, 3, KT, P], F32R, scope=mlp)
        fz = sb("fz", [P, 2, S], scope=mlp)
        fsplit = sb("fsplit", [P, FRING, 2, S], F32R, scope=mlp)
        gout = sb("gout", [P, KT, S], scope=mlp)
        scale_sb = sb("scale_sb", [P, 2 * MT + KT], scope=mlp)
        stats = sb("stats", [P, TT, 6], scope=mlp)
        mv = sb("mv", [P, TT, 2], scope=mlp)
        rs = sb("rs", [P, 6, TT], scope=mlp)
        rstd = sb("rstd", [P, NB, TT], scope=mlp)
        nmr = sb("nmr", [P, NB, TT], scope=mlp)
        mlp.close()

        q_r = sb("q_r", [P, 2, HG, S], F32R)
        k_r = sb("k_r", [P, 2, S], F32R)
        kn_r = sb("kn_r", [P, 2, VD, DH], F32R)
        v_r = sb("v_r", [P, 2, TT, DH], F32R)
        ow = sb("ow", [P, 2, HG, D], F32R)
        vt_sb = sb("vt_sb", [P, S])
        d_sb = sb("d_sb", [P, SRING, S])
        d_r = sb("d_r", [P, SRING, 2, S], F32R)
        o_r = sb("o_r", [P, 2, HG, S], F32R)
        acc = sb("acc", [P, NB, KT, S])
        rot1 = sb("rot1", [P, RRING, S])
        rot2 = sb("rot2", [P, RRING, S])
        st_r = sb("st_r", [P, 2, HG, DH], F32R)
        decay = sb("decay", [P, HG, 2, P])
        q_decay = sb("q_decay", [P, HG, HALF])
        fin = sb("fin", [P, 2, S])
        fin_in = stage[:].rearrange("p (r t) s -> p r t s", t=2)

        bank = [ctx.enter_context(nc.psum_tensor(f"bank{i}", [P, 512], F32)) for i in range(8)]
        down_ps = bank[0:4]
        gu_ps = bank[4:7]
        sc_ps = bank[0:3]
        o_ps = [bank[3], bank[6], bank[7], bank[3]]
        inter_ps = o_ps[0:2]
        proj_ps = [bank[4], bank[5], bank[0], bank[1], bank[2], bank[4]]
        out_ps = [bank[5], bank[0], bank[4], bank[5]]
        st_ps = bank[3]
        tail_ps = [[bank[5], bank[0], bank[4], bank[1]], [bank[2], bank[6], bank[7], bank[5]]]
        TAIL = [(half, u) for half in (1, 0) for u in range(KT)]

        def tail_in(u):
            return fin_in[:, u] if u < FINR else rot2[:, 0:2]

        def proj_bank(n, tile):
            return ([bank[4], bank[5], bank[6], bank[0], bank[1], bank[2]] if is_first(n) else proj_ps)[tile]

        def vt_bank(n):
            return bank[7] if is_first(n) else bank[6]

        def kt_bank(n):
            return bank[3] if is_first(n) else bank[7]

        def xn_tb(tb, part, k):
            if is_first(tb):
                return xn0[:, part, k, :]
            return xn123[:, tb - 1, part, k, :]

        x0_in = [sem(f"x0_in{i}") for i in range(TT)]
        x_in = [sem("x_in0"), sem("x_in1")]
        w_in = [sem(f"w_in{i}") for i in range(WRING)]
        const_in = sem("const_in"); ident_sem = sem("ident_sem"); rope_in = sem("rope_in")
        decay_in = sem("decay_in"); k_decay_in = sem("k_decay_in"); xn_in = sem("xn_in")
        aw_in = sem("aw_in"); ow_in = sem("ow_in"); gate_out = sem("gate_out"); xn_out = sem("xn_out")
        fin_ld = [sem(f"fin_ld{i}") for i in range(FINR)]
        stored = [sem("stored0"), sem("stored1")]
        tail_ld = sem("tail_ld"); tail_stored = sem("tail_stored")
        stats_d = sem("stats_d"); var_d = sem("var_d"); pow_c = sem("pow_c"); pow_d = sem("pow_d")
        newton = sem("newton"); rstd_d = sem("rstd_d")
        normed = sem("normed"); ln_t = sem("ln_t"); ln_hi = sem("ln_hi"); ln_lo = sem("ln_lo")
        k_exp = sem("k_exp"); k_made = sem("k_made"); k_added = sem("k_added"); w_ready = sem("w_ready")
        gu_done = sem("gu_done"); silu_d = sem("silu_d"); f_d = sem("f_d"); f_hi = sem("f_hi"); f_lo = sem("f_lo")
        down_d = sem("down_d"); gate_d = sem("gate_d")
        aw_hi = sem("aw_hi"); aw_lo = sem("aw_lo"); ow_hi = sem("ow_hi"); ow_lo = sem("ow_lo")
        proj_d = sem("proj_d"); turned = sem("turned"); rot_d = sem("rot_d"); qk_sum = sem("qk_sum")
        qk_hi = sem("qk_hi"); qk_lo = sem("qk_lo")
        vt_copied = sem("vt_copied"); vt_d = sem("vt_d"); v_hi = sem("v_hi"); v_lo = sem("v_lo")
        kt_d = sem("kt_d"); kn_hi = sem("kn_hi"); kn_lo = sem("kn_lo")
        score_d = sem("score_d"); decayed = sem("decayed"); q_decayed = sem("q_decayed")
        d_hi = sem("d_hi"); d_lo = sem("d_lo"); d_used = sem("d_used"); st_hi = sem("st_hi"); st_lo = sem("st_lo")
        o_hi = sem("o_hi"); o_lo = sem("o_lo"); out_d = sem("out_d"); zeroed = sem("zeroed"); acc_d = sem("acc_d")
        fin_p = sem("fin_p"); fin_d = sem("fin_d")
        tail_out = sem("tail_out"); tail_acc = sem("tail_acc"); tail_p = sem("tail_p"); tail_d = sem("tail_d")

        block = ctx.enter_context(nc.Block())

        def ln_ps(i):
            return down_ps[i] if i < TT else bank[7]

        def run_steps(eng, step):
            def group(g, final):
                step(g * NB, g, 0, start=True, final=final)
                with eng.Fori(1, NB - 1) as b:
                    step(b + g * NB, g, b, final=final)
                step(g * NB + (NB - 1), g, NB - 1, edge=not final, final=final, last=final)

            with eng.Fori(0, NG - 1) as g:
                group(g, False)
            group(NG - 1, True)

        @block.sync
        def _(sp):
            def load_x(tb):
                sp.dma_start(x_sb[:, tb % 2], x_nat[tb]).then_inc(x_in[tb % 2], 16)

            def load_w(q):
                if q >= WRING:
                    sp.wait_ge(w_ready, q - WRING + 1)
                sp.dma_start(stage[:, q % WRING, :], mlp_w[q // PARTS, :, q % PARTS, :]).then_inc(w_in[q % WRING], 16)

            def spill_xn(tb):
                sp.wait_ge(ln_lo, TT * (tb + 1))
                src = xn0[:] if tb == 0 else xn123[:, tb - 1]
                sp.dma_start(xn_dram[tb], src.bitcast(F32)).then_inc(xn_out, 16)

            def store_gates(tb):
                for d in range(KT):
                    sp.wait_ge(gate_d, tb * KT + d + 1)
                    sp.dma_start(g_dram[d, :, bass.ts(tb, S)], gout[:, d, :]).then_inc(gate_out, 16)

            def load_decay(g):
                sp.dma_start(decay[:], decay_tab[g]).then_inc(decay_in, 16)
                sp.dma_start(q_decay[:], q_decay_tab[g]).then_inc(decay_in, 16)

            def load_aw(g):
                sp.dma_start(stage[:], attn_w[g]).then_inc(aw_in, 16)

            for j in range(TT):
                sp.dma_start(x_sb[:, 0, j, :], x_nat[0, :, j, :]).then_inc(x0_in[j], 16)
            sp.dma_start(ident[:], ident_in).then_inc(ident_sem, 16)
            for q in range(3):
                load_w(q)
            sp.dma_start(scale_sb[:], scales).then_inc(const_in, 16)
            sp.dma_start(k_decay[:], k_decay_tab).then_inc(k_decay_in, 16)
            load_x(1)
            for q in range(3, NPARTS):
                load_w(q)
                if q == 14:
                    sp.wait_ge(ln_t, TT)
                    load_x(2)
            spill_xn(0)
            spill_xn(1)
            load_x(3)
            spill_xn(2)
            store_gates(0)
            sp.wait_ge(w_ready, NPARTS)
            load_aw(0)
            spill_xn(3)
            sp.dma_start(rope[:], rope_tab).then_inc(rope_in, 16)

            store_gates(1)
            with sp.Fori(2, NB) as tb:
                store_gates(tb)

            sp.wait_ge(down_d, NB * MT)
            sp.wait_ge(gate_out, 16 * KT * NB)
            load_decay(0)
            sp.wait_ge(aw_lo, PT)
            sp.dma_start(stage[:, 0:HG, :], out_w[0]).then_inc(ow_in, 16)
            sp.wait_ge(xn_out, 16 * NB)

            def load_xn(n, b):
                sp.wait_ge(proj_d, n * PT + PT)
                sp.dma_start(xn0[:].bitcast(F32), xn_dram[b]).then_inc(xn_in, 16)

            def load_fin(b, u):
                sp.dma_start(fin_in[:, u % FINR, 0, :], x_t[u, :, bass.ts(b, S)]).then_inc(fin_ld[u % FINR], 16)
                sp.dma_start(fin_in[:, u % FINR, 1, :], g_dram[u, :, bass.ts(b, S)]).then_inc(fin_ld[u % FINR], 16)

            def group(g, final):
                for b in range(NB):
                    n = g * NB + b
                    if b == NB - 1 and not final:
                        sp.wait_ge(decayed, n * NDEC + NDEC)
                        load_decay(g + 1)
                    if final:
                        if b == 0:
                            sp.wait_ge(ow_lo, g * HG + HG)
                        for u in range(FINR):
                            load_fin(b, u)
                    if b == 0 and not final:
                        sp.wait_ge(ow_lo, g * HG + HG)
                        load_aw(g + 1)
                    if b == NB - 1 and not final:
                        sp.wait_ge(aw_lo, g * PT + 2 * PT)
                        sp.dma_start(stage[:, 0:HG, :], out_w[g + 1]).then_inc(ow_in, 16)
                    if not (final and b >= NB - 2):
                        load_xn(n + 1, (b + 2) % NB)
                    if final and b < NB - 1:
                        for u in range(KT):
                            sp.wait_ge(fin_d, b * KT + u + 1)
                            sp.dma_start(out[u, :, bass.ts(b, S)], fin[:, u % 2, :]).then_inc(stored[u % 2], 16)
                            if u + FINR < KT:
                                load_fin(b, u + FINR)

            def last_stores():
                u, tokens = KT - 1, slice((NB - 1) * S, NB * S)
                sp.wait_ge(qk_sum, NG * NB * QK)
                sp.dma_start(tail_in(u)[:, 0, :], x_t[u, :, tokens]).then_inc(tail_ld, 16)
                sp.dma_start(tail_in(u)[:, 1, :], g_dram[u, :, tokens]).then_inc(tail_ld, 16)
                for k, (half, u) in enumerate(TAIL):
                    sp.wait_ge(tail_d, k + 1)
                    sp.dma_start(out[u, :, bass.ts((NB - 1) * 2 + half, HALF)],
                                 tail_in(u)[:, 0, bass.ts(half, HALF)]).then_inc(tail_stored, 16)

            load_xn(0, 1)
            with sp.Fori(0, NG - 1) as g:
                group(g, False)
            group(NG - 1, True)
            last_stores()
            for parity in range(2):
                sp.wait_ge(stored[parity], 8 * KT * (NB - 1))
            sp.wait_ge(tail_stored, 16 * len(TAIL))

        @block.scalar
        def _(act):
            def norm(i):
                tb, j = divmod(i, TT)
                act.wait_ge(rstd_d, tb + 1)
                act.activation(x_sb[:, tb % 2, j, :], x_sb[:, tb % 2, j, :], ACT.Identity,
                               bias=nmr[:, tb, j:j + 1], scale=rstd[:, tb, j:j + 1]).then_inc(normed, 1)

            def norm_hi(i):
                tb, j = divmod(i, TT)
                act.wait_ge(ln_t, i + 1)
                dst = xn0[:, 0, :, bass.ts(j, P)] if tb == 0 else xn123[:, tb - 1, 0, :, bass.ts(j, P)]
                act.copy(dst, ln_ps(i)[:].rearrange("p (k c) -> p k c", k=KT)).then_inc(ln_hi, 1)

            def silu_gate(tb, m):
                act.wait_ge(gu_done, tb * (2 * MT) + 2 * m + 1)
                if m >= 2 or not is_first(tb):
                    act.wait_ge(f_lo, tb * MT + m - 1)
                act.activation(fz[:, m % 2, :], gu_ps[(2 * m) % 3][:], ACT.Silu,
                               scale=scale_sb[:, m:m + 1]).then_inc(silu_d, 1)

            def fuse_hi(tb, m):
                act.wait_ge(f_d, tb * MT + m + 1)
                if m >= FRING or not is_first(tb):
                    act.wait_ge(down_d, tb * MT + m - FRING + 1)
                act.copy(fsplit[:, m % FRING, 0, :], fz[:, m % 2, :]).then_inc(f_hi, 1)

            def gates(tb):
                act.wait_ge(down_d, tb * MT + MT)
                if not is_first(tb):
                    act.wait_ge(gate_out, tb * (16 * KT))
                for d in range(KT):
                    act.activation(gout[:, d, :], down_ps[d][:], ACT.Silu,
                                   scale=scale_sb[:, 2 * MT + d:2 * MT + d + 1]).then_inc(gate_d, 1)

            def aw_split_hi(g, t):
                act.wait_ge(aw_in, g * 16 + 16)
                act.copy(aw[:, 0, t, :, :], stage[:, t, :]).then_inc(aw_hi, 1)

            for i in range(TT):
                norm(i)
            for i in range(TT):
                norm_hi(i)
            act.wait_ge(const_in, 16)
            for tb in range(2):
                for m in range(MT):
                    tile = LN_AT.get((tb, m))
                    silu_gate(tb, m)
                    if (tb, m + 1) in LN_AT:
                        norm(LN_AT[tb, m + 1])
                    fuse_hi(tb, m)
                    if tile is not None:
                        norm_hi(tile)
                    if tb >= 1 and m == FLAG - 1:
                        gates(tb - 1)
                    for t in AW_AT.get((tb, m), ()):
                        aw_split_hi(0, t)

            def ow_split_hi(g, h):
                act.wait_ge(ow_in, g * 16 + 16)
                if h == 0:
                    act.wait_ge(out_d, g * (NB * KT) + KT)
                act.copy(ow[:, 0, h, :], stage[:, h, :]).then_inc(ow_hi, 1)

            with act.Fori(2, NB) as tb:
                for m in range(MT):
                    silu_gate(tb, m)
                    fuse_hi(tb, m)
                    if m == FLAG - 1:
                        gates(tb - 1)
            act.wait_ge(down_d, NB * MT)
            act.wait_ge(xn_out, 16 * NB)

            def qk_round(n, r):
                first = is_first(n)
                act.wait_ge(qk_sum, n * QK + r + 1)
                if not first:
                    act.wait_ge(score_d, n * NBL)
                dst = k_r[:, 0, :] if r == 0 else q_r[:, 0, r - 1, :]
                act.copy(dst, rot1[:, r % RRING, :]).then_inc(qk_hi, 1)

            def turn(n, r):
                first = is_first(n)
                tile = 0 if r == 0 else r + 1
                ps = proj_bank(n, tile)
                act.wait_ge(proj_d, n * PT + tile + 1)
                if r >= RRING:
                    act.wait_ge(qk_sum, n * QK + r - RRING + 1)
                elif r == 0 and not first:
                    act.wait_ge(qk_sum, n * QK)
                act.copy(rot2[0:ROT, r % RRING, :], ps[ROT:, :])
                act.copy(rot2[ROT:, r % RRING, :], ps[0:ROT, :]).then_inc(turned, 1)

            def copy_vt(n):
                act.wait_ge(proj_d, n * PT + 2)
                if not is_first(n):
                    act.wait_ge(vt_d, n)
                act.copy(vt_sb[:], proj_bank(n, 1)[:]).then_inc(vt_copied, 1)

            def v_round(n):
                act.wait_ge(vt_d, n + 1)
                if not is_first(n):
                    act.wait_ge(d_used, n * NEL)
                act.copy(v_r[:, 0, :, :], vt_bank(n)[:].rearrange("p (t e) -> p t e", t=TT)).then_inc(v_hi, 1)

            def kn_round(n):
                act.wait_ge(kt_d, n + 1)
                act.copy(kn_r[:, 0, :, :], kt_bank(n)[:, 0:HALF].rearrange("p (t e) -> p t e", t=VD)).then_inc(kn_hi, 1)

            def st_round(n):
                act.wait_ge(d_used, n * NEL + VD)
                if is_first(n):
                    act.wait_ge(gate_out, 16 * KT * NB)
                act.copy(st_r[:, 0, :, :], st_ps[:].rearrange("p (h e) -> p h e", h=HG)).then_inc(st_hi, 1)

            def decayed_round(n, e):
                if VD <= e < SC:
                    act.wait_ge(q_decayed, n * HG + 2 * (e - VD) + 2)
                else:
                    act.wait_ge(decayed, n * NDEC + (e if e < VD else e - QD) + 1)
                if e >= SRING:
                    act.wait_ge(d_used, n * NEL + e - SRING + 1)
                else:
                    if_later(n, lambda: act.wait_ge(d_used, n * NEL + (e - SRING + 1)))
                act.copy(d_r[:, e % SRING, 0, :], d_sb[:, e % SRING, :]).then_inc(d_hi, 1)

            def projections(n, beside={}):
                for other in beside.get(0, ()):
                    other()
                copy_vt(n)
                for r in range(1, QK):
                    for other in beside.get(r, ()):
                        other()
                    turn(n, r)
                    qk_round(n, r - 1)
                    if r == 1:
                        v_round(n)
                        kn_round(n)
                    if r == 2:
                        for e in range(VD):
                            decayed_round(n, e)
                decayed_round(n, VD)
                qk_round(n, QK - 1)
                decayed_round(n, VD + 1)
                st_round(n)

            def o_round(n, i):
                act.wait_ge(d_used, n * NEL + SC + ODONE[i] + 1)
                if i == 0:
                    act.wait_ge(out_d, n * KT + KT)
                hs, qs = OTILES[i]
                act.copy(o_r[:, 0, hs, qs], o_ps[i][:].rearrange("p (h c) -> p h c", h=hs.stop - hs.start)).then_inc(o_hi, 1)

            def step(n, g, b, start=False, edge=False, final=False, last=False):
                for t in range(HEAD, NBL):
                    decayed_round(n, SC + t)
                    if edge and t == HEAD:
                        aw_split_hi(g + 1, 0)
                for i in range(2):
                    o_round(n, i)
                if edge:
                    aw_split_hi(g + 1, 1)
                elif not last:
                    turn(n + 1, 0)
                for i in range(2, NOT):
                    o_round(n, i)
                if edge:
                    aw_split_hi(g + 1, 2)
                    turn(n + 1, 0)
                if last:
                    return
                beside = {}
                if edge:
                    beside = {r: [lambda t=t: aw_split_hi(g + 1, t) for t in ts] for r, ts in ((0, (3, 4)), (1, (5,)))}
                if start:
                    beside = {r: [lambda h=h: ow_split_hi(g, h) for h in hs] for r, hs in ((0, (0, 1, 2)), (1, (3,)))}
                projections(n + 1, beside)
                for t in range(HEAD):
                    decayed_round(n + 1, SC + t)

            turn(0, 0)
            gates(NB - 1)
            projections(0)
            for t in range(HEAD):
                decayed_round(0, SC + t)
            run_steps(act, step)

        @block.vector
        def _(dve):
            def tile_stats(tb, j):
                if tb == 0:
                    dve.wait_ge(x0_in[j], 16)
                elif j == 0:
                    dve.wait_ge(x_in[tb % 2], 16 * ((tb + 1) // 2))
                    dve.wait_ge(rstd_d, tb)
                dve.bn_stats(stats[:, j, :], x_sb[:, tb % 2, j, :]).then_inc(stats_d, 1)

            def mean_var(tb):
                dve.wait_ge(stats_d, TT * (tb + 1))
                for j in range(TT):
                    dve.bn_aggr(mv[:, j, :], stats[:, j, :]).then_inc(newton, 1)
                dve.wait_ge(newton, 9 * tb + 4)
                dve.tensor_scalar(rs[:, 0, :], mv[:, :, 1], EPS, None, ALU.add).then_inc(var_d, 1)

            def inv_std(tb):
                dve.wait_ge(pow_d, tb + 1)
                c = 9 * tb + 4
                dve.tensor_tensor(rs[:, 3, :], rs[:, 2, :], rs[:, 2, :], ALU.mult).then_inc(newton, 1)
                dve.wait_ge(newton, c + 1)
                dve.tensor_tensor(rs[:, 4, :], rs[:, 3, :], rs[:, 0, :], ALU.mult).then_inc(newton, 1)
                dve.wait_ge(newton, c + 2)
                dve.tensor_scalar(rs[:, 5, :], rs[:, 4, :], -0.5, 1.5, ALU.mult, ALU.add).then_inc(newton, 1)
                dve.wait_ge(newton, c + 3)
                dve.tensor_tensor(rstd[:, tb, :], rs[:, 5, :], rs[:, 2, :], ALU.mult).then_inc(newton, 1)
                dve.wait_ge(newton, c + 4)
                dve.tensor_tensor(rs[:, 3, :], mv[:, :, 0], rstd[:, tb, :], ALU.mult).then_inc(newton, 1)
                dve.wait_ge(newton, c + 5)
                dve.tensor_scalar(nmr[:, tb, :], rs[:, 3, :], -1.0, None, ALU.mult).then_inc(rstd_d, 1)

            def norm_lo(i):
                tb, j = divmod(i, TT)
                dve.wait_ge(ln_hi, i + 1)
                parts = xn0 if tb == 0 else xn123[:, tb - 1]
                hi = parts[:, 0, :, bass.ts(j, P)]
                lo = parts[:, 1, :, bass.ts(j, P)]
                dve.tensor_tensor(lo, ln_ps(i)[:].rearrange("p (k c) -> p k c", k=KT), hi.bitcast(F32),
                                  ALU.subtract).then_inc(ln_lo, 1)

            def w_exponent(q):
                dve.wait_ge(w_in[q % WRING], 16 * (q // WRING + 1))
                if q >= MRING:
                    dve.wait_ge(w_ready, q - MRING + 1)
                dve.tensor_scalar(magic[:, q % MRING, :].bitcast(I32), stage[:, q % WRING, :].bitcast(I32),
                                  EXP_MASK, None, ALU.bitwise_and).then_inc(k_exp, 1)

            def w_magic(q):
                dve.wait_ge(k_exp, q + 1)
                dve.tensor_scalar(magic[:, q % MRING, :], magic[:, q % MRING, :], F8_SCALE, F8_FLOOR,
                                  ALU.mult, ALU.max).then_inc(k_made, 1)

            def w_round(q):
                dve.wait_ge(k_added, q + 1)
                dve.tensor_tensor(gu_w[:, q // PARTS, q % PARTS, :, :],
                                  stage[:, q % WRING, :].rearrange("p (k c) -> p k c", k=KT),
                                  magic[:, q % MRING, :].rearrange("p (k c) -> p k c", k=KT),
                                  ALU.subtract).then_inc(w_ready, 1)

            def fuse(tb, m):
                dve.wait_ge(gu_done, tb * (2 * MT) + 2 * m + 2)
                dve.wait_ge(silu_d, tb * MT + m + 1)
                dve.scalar_tensor_tensor(out=fz[:, m % 2, :], in0=gu_ps[(2 * m + 1) % 3][:],
                                         scalar=scale_sb[:, MT + m:MT + m + 1], in1=fz[:, m % 2, :],
                                         op0=ALU.mult, op1=ALU.mult).then_inc(f_d, 1)

            def aw_split_lo(g, t):
                dve.wait_ge(aw_hi, g * PT + t + 1)
                dve.tensor_tensor(aw[:, 1, t, :, :],
                                  stage[:, t, :].rearrange("p (k c) -> p k c", k=KT),
                                  aw[:, 0, t, :, :].bitcast(F32), ALU.subtract).then_inc(aw_lo, 1)

            for j in range(TT):
                tile_stats(0, j)
            mean_var(0)
            w_exponent(0)
            w_magic(0)
            inv_std(0)

            def w_step(q):
                if q + MLEAD < NPARTS:
                    w_exponent(q + MLEAD)
                w_round(q)
                if q + MLEAD < NPARTS:
                    w_magic(q + MLEAD)

            for q in range(1, MLEAD):
                w_exponent(q)
                w_magic(q)
            w_step(0)
            for i in range(TT):
                norm_lo(i)
            for q in range(1, PARTS):
                w_step(q)
            dve.wait_ge(const_in, 16)
            for tb in range(2):
                for m in range(MT):
                    if tb == 0 and m + 1 < MT:
                        for q in range(PARTS * (m + 1), PARTS * (m + 2)):
                            w_step(q)
                    if (tb, m) == (0, TT):
                        inv_std(1)
                    fuse(tb, m)
                    if tb == 0 and m < TT:
                        tile_stats(1, m)
                    if (tb, m) == (0, TT - 1):
                        mean_var(1)
                    if tb == 0 and (tb, m - 1) in LN_AT:
                        norm_lo(LN_AT[tb, m - 1])
                    if (tb == 1 or m == MT - 1) and (tb, m) in LN_AT:
                        norm_lo(LN_AT[tb, m])
                    if (tb, m) in ((0, MT - 1), (1, 2)):
                        for j in range(TT):
                            tile_stats(2 + tb, j)
                        mean_var(2 + tb)
                    if (tb, m) in ((1, 0), (1, 3)):
                        inv_std(2 + m // 3)
                    for t in AW_AT.get((tb, m), ()):
                        aw_split_lo(0, t)

            def ow_split_lo(g, h):
                dve.wait_ge(ow_hi, g * HG + h + 1)
                dve.tensor_tensor(ow[:, 1, h, :], stage[:, h, :], ow[:, 0, h, :].bitcast(F32),
                                  ALU.subtract).then_inc(ow_lo, 1)

            with dve.Fori(2, NB) as tb:
                for m in range(MT):
                    fuse(tb, m)
            dve.wait_ge(down_d, NB * MT)
            dve.wait_ge(xn_out, 16 * NB)
            dve.wait_ge(rope_in, 16)
            dve.wait_ge(k_decay_in, 16)

            def rotate(n, r):
                first = is_first(n)
                tile = 0 if r == 0 else r + 1
                dve.wait_ge(turned, n * QK + r + 1)
                if r >= RRING:
                    dve.wait_ge(qk_lo, n * QK + r - RRING + 1)
                    if r == RRING:
                        dve.wait_ge(kt_d, n + 1)
                    else:
                        dve.wait_ge(q_decayed, n * HG + r - RRING)
                elif r == 0 and not first:
                    dve.wait_ge(qk_lo, n * QK)
                    dve.wait_ge(q_decayed, n * HG)
                dve.tensor_tensor(rot1[:, r % RRING, :], proj_bank(n, tile)[:], rope[:, 0, :], ALU.mult)
                dve.tensor_tensor(rot2[:, r % RRING, :], rot2[:, r % RRING, :], rope[:, 1, :],
                                  ALU.mult).then_inc(rot_d, 1)

            def qk_rest(n, r):
                dve.wait_ge(qk_hi, n * QK + r + 1)
                dst, hi = (k_r[:, 1, :], k_r[:, 0, :]) if r == 0 else (q_r[:, 1, r - 1, :], q_r[:, 0, r - 1, :])
                dve.tensor_tensor(dst, rot1[:, r % RRING, :], hi.bitcast(F32), ALU.subtract).then_inc(qk_lo, 1)

            def v_rest(n):
                dve.wait_ge(v_hi, n + 1)
                dve.tensor_tensor(v_r[:, 1, :, :], vt_bank(n)[:].rearrange("p (t e) -> p t e", t=TT),
                                  v_r[:, 0, :, :].bitcast(F32), ALU.subtract).then_inc(v_lo, 1)

            def v_decay(n, g, j):
                if_later(n, lambda: dve.wait_ge(d_lo, n * NEL + (j - SRING + 1)))
                dve.tensor_tensor(d_sb[:, j, :].rearrange("p (h e) -> p h e", h=HG),
                                  vt_bank(n)[:, bass.ts(j, P)].unsqueeze(1).broadcast_to([P, HG, DH]),
                                  k_decay[:, g, j, :].unsqueeze(2).broadcast_to([P, HG, DH]), ALU.mult).then_inc(decayed, 1)

            def q_decay_head(n, h):
                e = VD + h // 2
                if h % 2 == 0:
                    if_later(n, lambda: dve.wait_ge(d_lo, n * NEL + (e - SRING + 1)))
                dve.tensor_tensor(d_sb[:, e, bass.ts(h % 2, HALF)], rot1[:, (h + 1) % RRING, HALF:S],
                                  q_decay[:, h, :], ALU.mult).then_inc(q_decayed, 1)

            def kn_rest(n):
                dve.wait_ge(kn_hi, n + 1)
                dve.tensor_tensor(kn_r[:, 1, :, :], kt_bank(n)[:, 0:HALF].rearrange("p (t e) -> p t e", t=VD),
                                  kn_r[:, 0, :, :].bitcast(F32), ALU.subtract).then_inc(kn_lo, 1)

            def st_rest(n):
                dve.wait_ge(st_hi, n + 1)
                dve.tensor_tensor(st_r[:, 1, :, :], st_ps[:].rearrange("p (h e) -> p h e", h=HG),
                                  st_r[:, 0, :, :].bitcast(F32), ALU.subtract).then_inc(st_lo, 1)

            def projections(n, g, tables=None, beside={}):
                for other in beside.get(0, ()):
                    other()
                for r in range(1, QK):
                    for other in beside.get(r, ()):
                        other()
                    rotate(n, r)
                    qk_rest(n, r - 1)
                    if r == 1:
                        v_rest(n)
                        for j in range(VD):
                            v_decay(n, g, j)
                        kn_rest(n)
                    if r == 2 and tables is not None:
                        dve.wait_ge(decay_in, tables * 32 + 32)
                    if r >= 2:
                        q_decay_head(n, r - 2)
                qk_rest(n, QK - 1)
                q_decay_head(n, HG - 1)

            def decay_block(n, t):
                j, h0, nh, i0, ni = BLOCKS[t]
                e = SC + t
                dve.wait_ge(score_d, n * NBL + t + 1)
                if e >= SRING:
                    dve.wait_ge(d_lo, n * NEL + e - SRING + 1)
                else:
                    if_later(n, lambda: dve.wait_ge(d_lo, n * NEL + (e - SRING + 1)))
                by_head = lambda ap: ap.rearrange("p (h i c) -> p h i c", h=nh, i=ni)
                dve.tensor_tensor(by_head(d_sb[:, e % SRING, :]), by_head(sc_ps[t % TRING][:]),
                                  decay[:, h0:h0 + nh, i0 - j:i0 - j + ni, :], ALU.mult).then_inc(decayed, 1)

            def o_rest(n, i):
                dve.wait_ge(o_hi, n * NOT + i + 1)
                hs, qs = OTILES[i]
                dve.tensor_tensor(o_r[:, 1, hs, qs], o_ps[i][:].rearrange("p (h c) -> p h c", h=hs.stop - hs.start),
                                  o_r[:, 0, hs, qs].bitcast(F32), ALU.subtract).then_inc(o_lo, 1)

            def accumulate(n, b, u):
                dve.wait_ge(out_d, n * KT + KT + u + 1)
                dve.tensor_tensor(acc[:, b, u, :], out_ps[u][:], acc[:, b, u, :], ALU.add).then_inc(acc_d, 1)

            def finish(n, b, u):
                dve.wait_ge(acc_d, n * KT + KT + u + 1)
                loads = len(range(u % FINR, KT, FINR))
                dve.wait_ge(fin_ld[u % FINR], b * (32 * loads) + (u // FINR + 1) * 32)
                dve.tensor_tensor(fin_in[:, u % FINR, 1, :], acc[:, b, u, :], fin_in[:, u % FINR, 1, :],
                                  ALU.mult).then_inc(fin_p, 1)
                dve.wait_ge(fin_p, b * KT + u + 1)
                if u >= 2:
                    dve.wait_ge(stored[u % 2], (b * (KT // 2) + u // 2) * 16)
                else:
                    if_later(b, lambda: dve.wait_ge(stored[u % 2], b * (KT // 2) * 16))
                dve.tensor_tensor(fin[:, u % 2, :], fin_in[:, u % FINR, 1, :], fin_in[:, u % FINR, 0, :],
                                  ALU.add).then_inc(fin_d, 1)

            def tail_piece(k):
                half, u = TAIL[k]
                b, cols = NB - 1, bass.ts(half, HALF)
                x, gate = tail_in(u)[:, 0, cols], tail_in(u)[:, 1, cols]
                dve.wait_ge(tail_out, k + 1)
                dve.tensor_tensor(acc[:, b, u, cols], tail_ps[k // KT][u][:, 0:HALF], acc[:, b, u, cols],
                                  ALU.add).then_inc(tail_acc, 1)
                if u < FINR:
                    dve.wait_ge(fin_ld[u], b * (32 * len(range(u, KT, FINR))) + 32)
                else:
                    dve.wait_ge(tail_ld, 32)
                dve.wait_ge(tail_acc, k + 1)
                dve.tensor_tensor(gate, acc[:, b, u, cols], gate, ALU.mult).then_inc(tail_p, 1)
                dve.wait_ge(tail_p, k + 1)
                dve.tensor_tensor(x, gate, x, ALU.add).then_inc(tail_d, 1)

            def step(n, g, b, start=False, edge=False, final=False, last=False):
                for t in range(HEAD, NBL):
                    decay_block(n, t)
                    if edge and t == HEAD:
                        aw_split_lo(g + 1, 0)
                if final and not start:
                    finish(n - 1, b - 1, KT - 1)
                for i in range(2):
                    o_rest(n, i)
                if edge:
                    aw_split_lo(g + 1, 1)
                elif not last:
                    rotate(n + 1, 0)
                for i in range(2, NOT):
                    o_rest(n, i)
                if edge:
                    aw_split_lo(g + 1, 2)
                    rotate(n + 1, 0)
                if not last:
                    beside = {}
                    if edge:
                        beside = {r: [lambda t=t: aw_split_lo(g + 1, t) for t in ts] for r, ts in ((0, (3, 4)), (1, (5,)))}
                    if start:
                        beside = {r: [lambda h=h: ow_split_lo(g, h) for h in hs] for r, hs in ((0, (0, 1, 2)), (1, (3,)))}
                    projections(n + 1, g + 1 if edge else g, g + 1 if edge else None, beside)
                if last:
                    for k in range(len(TAIL)):
                        tail_piece(k)
                    return
                for u in range(KT):
                    if u == 2:
                        st_rest(n + 1)
                    if u == KT - 1:
                        for t in range(HEAD):
                            decay_block(n + 1, t)
                    accumulate(n, b, u)
                    if final and u < KT - 1:
                        finish(n, b, u)

            rotate(0, 0)
            projections(0, 0, 0)
            st_rest(0)
            for t in range(HEAD):
                decay_block(0, t)
            dve.wait_ge(zeroed, NB)
            dve.sem_inc(acc_d, KT)
            dve.sem_inc(out_d, KT)
            run_steps(dve, step)

        @block.gpsimd
        def _(pool):
            pool.memset(rs[:, 1, :], -0.5).then_inc(pow_c, 1)
            pool.wait_ge(pow_c, 1)

            def power(tb):
                pool.wait_ge(var_d, tb + 1)
                if tb >= 1:
                    pool.wait_ge(rstd_d, tb)
                pool.tensor_tensor(rs[:, 2, :], rs[:, 0, :], rs[:, 1, :], ALU.pow).then_inc(pow_d, 1)

            def w_add(q):
                pool.wait_ge(k_made, q + 1)
                pool.tensor_tensor(stage[:, q % WRING, :], stage[:, q % WRING, :], magic[:, q % MRING, :],
                                   ALU.add).then_inc(k_added, 1)

            def fuse_rest(tb, m):
                pool.wait_ge(f_hi, tb * MT + m + 1)
                pool.tensor_tensor(fsplit[:, m % FRING, 1, :], fz[:, m % 2, :], fsplit[:, m % FRING, 0, :].bitcast(F32),
                                   ALU.subtract).then_inc(f_lo, 1)

            power(0)
            for q in range(PARTS + MLEAD):
                w_add(q)
            for tb in range(2):
                for m in range(MT):
                    if (tb, m) == (0, TT):
                        power(1)
                    if tb == 0:
                        for q in range(PARTS * (m + 1) + MLEAD, min(PARTS * (m + 2) + MLEAD, NPARTS)):
                            w_add(q)
                    if (tb, m) in ((1, 0), (1, 3)):
                        power(2 + m // 3)
                    fuse_rest(tb, m)
            with pool.Fori(2, NB) as tb:
                for m in range(MT):
                    fuse_rest(tb, m)

            pool.wait_ge(down_d, NB * MT)

            def zero(b):
                pool.memset(acc[:, b], 0.0).then_inc(zeroed, 1)

            def decayed_rest(n, e):
                pool.wait_ge(d_hi, n * NEL + e + 1)
                pool.tensor_tensor(d_r[:, e % SRING, 1, :], d_sb[:, e % SRING, :],
                                   d_r[:, e % SRING, 0, :].bitcast(F32), ALU.subtract).then_inc(d_lo, 1)

            def projections(n, beside={}):
                for r in range(QK):
                    for other in beside.get(r, ()):
                        other()
                    pool.wait_ge(rot_d, n * QK + r + 1)
                    pool.tensor_tensor(rot1[:, r % RRING, :], rot1[:, r % RRING, :], rot2[:, r % RRING, :],
                                       ALU.add).then_inc(qk_sum, 1)
                    if r == 2:
                        for e in range(VD):
                            decayed_rest(n, e)
                for e in range(VD, SC):
                    decayed_rest(n, e)

            def step(n, g, b, start=False, edge=False, final=False, last=False):
                for t in range(HEAD, NBL):
                    decayed_rest(n, SC + t)
                if last:
                    return
                projections(n + 1)
                for t in range(HEAD):
                    decayed_rest(n + 1, SC + t)

            projections(0, {r: [lambda b=b: zero(b) for b in bs] for r, bs in ((0, (0, 1)), (1, (2,)), (2, (3,)))})
            for t in range(HEAD):
                decayed_rest(0, SC + t)
            run_steps(pool, step)

        @block.tensor
        def _(pe):
            def products(dst, pairs, start=True, stop=True):
                for x, (a, b) in enumerate(pairs):
                    last = pe.matmul(dst, a, b, start=start and x == 0, stop=stop and x == len(pairs) - 1)
                return last

            def ln_transpose(i):
                pe.wait_ge(normed, i + 1)
                if i > TT:
                    pe.wait_ge(ln_lo, i)
                for k in range(KT):
                    last = pe.transpose(ln_ps(i)[:, bass.ts(k, P)], x_sb[:, i // TT % 2, i % TT, bass.ts(k, P)], ident[:])
                last.then_inc(ln_t, 1)

            def gate_up(tb, m, s):
                q = 2 * m + s
                first = is_first(tb)
                if not first or q >= 3:
                    was = q - 3
                    pe.wait_ge(f_d if was % 2 else silu_d, tb * MT + was // 2 + 1)
                for part in range(2):
                    if first and q == 0 and part == 1:
                        pe.wait_ge(ln_lo, TT)
                    last = products(gu_ps[q % 3][:], [(gu_w[:, m, s, k, :], xn_tb(tb, part, k)) for k in range(KT)],
                                    start=(part == 0), stop=(part == 1))
                last.then_inc(gu_done, 1)

            def down(tb, m):
                pe.wait_ge(f_lo, tb * MT + m + 1)
                if is_first(tb):
                    pe.wait_ge(w_ready, PARTS * (m + 1))
                if m == 0 and is_first(tb):
                    pe.wait_ge(ln_lo, TT)
                elif m == 0:
                    pe.wait_ge(gate_d, tb * KT)
                for d in range(KT):
                    last = products(down_ps[d][:], [(gu_w[:, m, 2, d, :], fsplit[:, m % FRING, part, :]) for part in range(2)],
                                    start=(m == 0), stop=(m == MT - 1))
                last.then_inc(down_d, 1)

            pe.wait_ge(ident_sem, 16)
            for i in range(TT):
                ln_transpose(i)
            pe.wait_ge(ln_hi, TT)
            for tb in range(2):
                if tb == 1:
                    pe.wait_ge(ln_lo, 2 * TT)
                for m in range(MT):
                    for part in range(2):
                        if tb == 0:
                            pe.wait_ge(w_ready, PARTS * m + part + 1)
                        gate_up(tb, m, part)
                    if (tb, m) in LN_AT:
                        ln_transpose(LN_AT[tb, m])
                    if m >= FLAG:
                        down(tb, m - FLAG)
                    elif tb >= 1:
                        down(tb - 1, m - FLAG + MT)
            pe.wait_ge(ln_lo, NB * TT)
            with pe.Fori(2, NB) as tb:
                for m in range(MT):
                    gate_up(tb, m, 0)
                    gate_up(tb, m, 1)
                    if m >= FLAG:
                        down(tb, m - FLAG)
                    else:
                        down(tb - 1, m - FLAG + MT)

            SPLIT = [(0, 0), (0, 1), (1, 0)]

            def project(n, tile, g_edge=None):
                first = is_first(n)
                if g_edge is not None:
                    pe.wait_ge(aw_lo, g_edge * PT + tile + 1)
                if tile == 0 and not first:
                    pe.wait_ge(xn_in, n * 16)
                if tile < 2 and not first:
                    pe.wait_ge(acc_d, (n - 1) * KT + 3 + tile)
                elif 2 <= tile < PT - 1 and not first:
                    pe.wait_ge(decayed, n * NDEC)
                elif tile == PT - 1 and not first:
                    pe.wait_ge(rot_d, n * QK + 1)
                products(proj_bank(n, tile)[:], [(aw[:, a, tile, k, :], xn0[:, c, k, :])
                                            for a, c in SPLIT for k in range(KT)]).then_inc(proj_d, 1)

            def transpose_v(n):
                pe.wait_ge(vt_copied, n + 1)
                if not is_first(n):
                    pe.wait_ge(o_lo, (n - 1) * NOT + 2)
                for j in range(TT):
                    last = pe.transpose(vt_bank(n)[:, bass.ts(j, P)], vt_sb[:, bass.ts(j, P)], ident[:])
                last.then_inc(vt_d, 1)

            def transpose_k(n):
                pe.wait_ge(qk_sum, n * QK + 1)
                if not is_first(n):
                    pe.wait_ge(o_lo, (n - 1) * NOT + 3)
                for j in range(VD):
                    last = pe.transpose(kt_bank(n)[:, bass.ts(j, P)], rot1[:, 0, bass.ts(j, P)], ident[:])
                last.then_inc(kt_d, 1)

            def state(n):
                pe.wait_ge(kn_lo, n + 1)
                if_later(n, lambda: pe.wait_ge(o_lo, n * NOT))
                for j in range(VD):
                    pe.wait_ge(d_lo, n * NEL + j + 1)
                    products(st_ps[:], [(kn_r[:, a, j, :], d_r[:, j, c, :]) for a, c in SPLIT],
                                    start=(j == 0), stop=(j == VD - 1)).then_inc(d_used, 1)

            def inter(n):
                pe.wait_ge(st_lo, n + 1)
                pe.wait_ge(decayed, n * NDEC + VD)
                for x in range(QD):
                    pe.wait_ge(d_lo, n * NEL + VD + x + 1)
                    tile = inter_ps[x][:].rearrange("p (h c) -> p h c", h=2)
                    for h in range(2):
                        last = products(tile[:, h, :], [(st_r[:, a, 2 * x + h, :], d_r[:, VD + x, c, bass.ts(h, HALF)])
                                                        for a, c in SPLIT], start=(h == 0), stop=False)
                    last.then_inc(d_used, 1)

            def projections(n, g_edge=None, skip_first=1):
                for tile in range(skip_first, PT):
                    project(n, tile, g_edge)
                    if tile == 2:
                        transpose_v(n)
                        transpose_k(n)

            def scores(n, t):
                j, h0, nh, i0, ni = BLOCKS[t]
                if t >= TRING:
                    pe.wait_ge(decayed, n * NDEC + VD + t - TRING + 1)
                elif t == 0:
                    pe.wait_ge(qk_lo, n * QK + QK)
                    if_later(n, lambda: pe.wait_ge(acc_d, n * KT + 2))
                products(sc_ps[t % TRING][:], [(k_r[:, a, bass.ts(j, P)], q_r[:, c, h0:h0 + nh, i0 * P:(i0 + ni) * P])
                                               for a, c in SPLIT]).then_inc(score_d, 1)

            def times_v(n, t):
                j, h0, nh, i0, ni = BLOCKS[t]
                e = SC + t
                pairs = lambda cols: [(v_r[:, a, j, :], d_r[:, e % SRING, c, cols]) for a, c in SPLIT]
                if t == 0:
                    pe.wait_ge(v_lo, n + 1)
                if t == NBL - 1:
                    pe.wait_ge(o_lo, n * NOT + 1)
                pe.wait_ge(d_lo, n * NEL + e + 1)
                if t == 0:
                    for x in range(2):
                        tile = o_ps[x][:].rearrange("p (h c) -> p h c", h=2)[:, :, P:HALF]
                        last = products(tile, pairs(slice(x * HALF, (x + 1) * HALF)), start=False, stop=False)
                    last.then_inc(d_used, 1)
                else:
                    x = OF_BLOCK[t]
                    products(o_ps[x][:], pairs(slice(0, S)), start=t in (3, 5), stop=t in ODONE).then_inc(d_used, 1)

            def last_out_projection(n):
                pe.wait_ge(acc_d, n * KT + KT)
                for k, (half, u) in enumerate(TAIL):
                    if u == 0:
                        pe.wait_ge(o_lo, n * NOT + (NOT if half == 0 else 2))
                    if k == len(TAIL) - 1:
                        pe.wait_ge(tail_acc, 1)
                    products(tail_ps[k // KT][u][:, 0:HALF], [(ow[:, a, h, bass.ts(u, P)], o_r[:, c, h, bass.ts(half, HALF)])
                                                              for h in range(HG) for a, c in SPLIT]).then_inc(tail_out, 1)

            def out_projection(n, g, u):
                if u == 0:
                    pe.wait_ge(vt_copied, n + 2)
                elif u == 1:
                    pe.wait_ge(rot_d, n * QK + QK + 2)
                elif u == 2:
                    pe.wait_ge(rot_d, n * QK + 2 * QK)
                else:
                    pe.wait_ge(acc_d, n * KT + KT + 1)
                products(out_ps[u][:], [(ow[:, a, h, bass.ts(u, P)], o_r[:, c, h, :])
                                        for h in range(HG) for a, c in SPLIT]).then_inc(out_d, 1)

            def step(n, g, b, start=False, edge=False, final=False, last=False):
                g_edge = g + 1 if edge else None
                for t in range(HEAD, NBL + LAG):
                    if t < NBL:
                        scores(n, t)
                    if t == NBL and not last:
                        project(n + 1, 0, g_edge)
                    if t >= LAG:
                        times_v(n, t - LAG)
                if last:
                    last_out_projection(n)
                    return
                projections(n + 1, g_edge)
                pe.wait_ge(o_lo, n * NOT + NOT)
                if start:
                    pe.wait_ge(ow_lo, g * HG + HG)
                for u in range(KT):
                    if u == 2:
                        state(n + 1)
                    if u == KT - 1:
                        for t in range(HEAD):
                            scores(n + 1, t)
                        inter(n + 1)
                    out_projection(n, g, u)

            pe.wait_ge(f_d, NB * MT - 1)
            down(NB - 1, MT - 2)
            project(0, 0, 0)
            down(NB - 1, MT - 1)
            pe.wait_ge(silu_d, NB * MT)
            pe.wait_ge(f_d, NB * MT)
            project(0, 1, 0)
            project(0, 2, 0)
            pe.wait_ge(gate_d, NB * KT)
            transpose_v(0)
            transpose_k(0)
            projections(0, 0, skip_first=3)
            state(0)
            for t in range(HEAD):
                scores(0, t)
            inter(0)
            run_steps(pe, step)


def is_first(n):
    return isinstance(n, int) and n == 0


def if_later(n, wait):
    if not is_first(n):
        wait()


def _constants():
    import numpy as np
    f = np.float32
    inv = f(1.0) / np.power(f(10000.0), np.arange(0, DH, 2, dtype=f) / f(DH)).astype(f)
    angle = (np.arange(S, dtype=f)[:, None] * inv[None, :]).astype(f).T.astype(np.float64)
    cos, sin = np.cos(angle), np.sin(angle)
    rope = np.stack([np.concatenate([cos, cos]), np.concatenate([-sin, sin])], axis=1).astype(f)
    lam = np.exp2(-8.0 * np.arange(1, H + 1, dtype=np.float64) / H)
    j = np.arange(P)[:, None, None]
    dist = P * np.arange(2)[None, :, None] + np.arange(P)[None, None, :] - j
    table = np.where(dist >= 0, np.exp(-lam[:, None, None, None] * np.maximum(dist, 0)), 0.0)
    decay = table.reshape(NG, HG, P, 2, P).transpose(0, 2, 1, 3, 4).astype(f)
    q_decay = np.exp(-lam[:, None] * np.arange(1, HALF + 1)).reshape(NG, 1, HG, HALF)
    q_decay = np.broadcast_to(q_decay, (NG, P, HG, HALF)).astype(f)
    k_decay = np.exp(-lam[:, None] * np.arange(HALF - 1, -1, -1)).reshape(NG, HG, VD, P).transpose(3, 0, 2, 1).astype(f)
    c = np.ascontiguousarray
    return rope, c(decay), c(q_decay), c(k_decay), np.eye(P, dtype=f)


def kernel(L0_attn_x, L0_attn_wq, L0_attn_wk, L0_attn_wv, L0_attn_wo, L0_ffn_gate_w, L0_ffn_up_w, L0_ffn_down_w,
           L0_ffn_gate_scale, L0_ffn_up_scale, L0_ffn_down_scale):
    import numpy as np
    import concourse.bacc as bacc
    from concourse.bass_utils import run_bass_kernel_spmd

    c = np.ascontiguousarray
    x = np.asarray(L0_attn_x)
    x_nat = c(x.reshape(NB, TT, P, D).transpose(0, 2, 1, 3))
    x_t = c(x.reshape(NB * S, KT, P).transpose(1, 2, 0))
    wq = np.asarray(L0_attn_wq).reshape(NG, HG, DH, KT, P)
    wk = np.asarray(L0_attn_wk).reshape(NG, 1, DH, KT, P)
    wv = np.asarray(L0_attn_wv).reshape(NG, 1, DH, KT, P)
    attn_w = c(np.concatenate([wk, wv, wq], axis=1).transpose(0, 4, 1, 3, 2).reshape(NG, P, PT, KT * P))
    out_w = c(np.asarray(L0_attn_wo).reshape(D, NG, HG, P).transpose(1, 3, 2, 0))
    gu = [np.asarray(w).reshape(KT, P, MT, P).transpose(2, 1, 0, 3) for w in (L0_ffn_gate_w, L0_ffn_up_w)]
    dw = np.asarray(L0_ffn_down_w).reshape(MT, P, KT, P)
    mlp_w = c(np.stack(gu + [dw], axis=2).reshape(MT, P, PARTS, KT * P))
    scales = c(np.concatenate([np.asarray(L0_ffn_gate_scale).reshape(MT, P), np.asarray(L0_ffn_up_scale).reshape(MT, P),
                               np.asarray(L0_ffn_down_scale).reshape(KT, P)]).T)
    rope, decay, q_decay, k_decay, ident = _constants()
    arrays = {"x_nat": x_nat, "x_t": x_t, "attn_w": attn_w, "out_w": out_w, "mlp_w": mlp_w, "scales": scales,
              "rope": rope, "decay": decay, "q_decay": q_decay, "k_decay": k_decay, "ident": ident}

    nc = bacc.Bacc("TRN2", target_bir_lowering=False, num_devices=1)
    args = [nc.dram_tensor(f"in_{k}", a.shape, F32, kind="ExternalInput").ap() for k, a in arrays.items()]
    out = nc.dram_tensor("out_t", (KT, P, NB * S), F32, kind="ExternalOutput").ap()
    attention_mlp_kernel(nc, *args, out)
    r = run_bass_kernel_spmd(nc, [{f"in_{k}": a for k, a in arrays.items()}], core_ids=[0])
    got = r.results[0]["out_t"]
    return got.reshape(D, NB, S).transpose(1, 2, 0)
```
